# Optimizing a Trainium2 kernel written in Bass

```python
import numpy as np
import jax
import jax.numpy as jnp

def _softmax(x, axis=-1):
    return jax.nn.softmax(x, axis=axis)

def _gelu(x):
    return jax.nn.gelu(x, approximate=True)

def _silu(x):
    return jax.nn.silu(x)

def _sigmoid(x):
    return jax.nn.sigmoid(x)

def _layernorm(x, axis=-1, eps=1e-05):
    m = jnp.mean(x, axis=axis, keepdims=True)
    v = jnp.var(x, axis=axis, keepdims=True)
    return (x - m) / jnp.sqrt(v + eps)

def _scatter_add(tgt, idx, src, axis=0):
    return tgt.at[idx].add(src)

def _segment_sum(src, seg, n):
    return jax.ops.segment_sum(src, seg, n)
kernel_name = 'mk_seq_preln_d1_jaxref_r8_30cbd6'

def setup_inputs(seed: int=0):
    np.random.seed(seed)
    _w = jnp.asarray

    def _L0_attn_setup():
        import jax, jax.numpy as jnp
        import numpy as np
        DIM = 128
        B, N = (8, 512)
        EPS = 1e-06
        key = jax.random.key(seed)
        k1, k2, k3, k4 = jax.random.split(key, 4)
        x = jax.random.normal(k1, (B, N, DIM), dtype=jnp.float32)
        s = 1.0 / np.sqrt(DIM)
        W_qkv = jax.random.uniform(k2, (3 * DIM, DIM), jnp.float32, -s, s)
        W_out = jax.random.uniform(k3, (DIM, DIM), jnp.float32, -s, s)
        b_out = jax.random.uniform(k4, (DIM,), jnp.float32, -s, s)
        return {'x': x, 'W_qkv': W_qkv, 'W_out': W_out, 'b_out': b_out}
    _L0_attn_in = _L0_attn_setup()

    def _L0_ffn_setup():
        import math
        import jax, jax.numpy as jnp
        from jax import lax
        import numpy as np
        E = 16
        K = 2
        CF = 1.25
        key = jax.random.key(seed)
        k0, k1, k2, k3, k4 = jax.random.split(key, 5)
        B, S, D, H = (2, 256, 128, 128)
        scale = 0.02
        return {'x': jax.random.normal(k0, (B, S, D), dtype=jnp.float32), 'router_w': jax.random.normal(k1, (D, E), dtype=jnp.float32) * scale, 'gate_w': jax.random.normal(k2, (E, D, H), dtype=jnp.float32) * scale, 'up_w': jax.random.normal(k3, (E, D, H), dtype=jnp.float32) * scale, 'down_w': jax.random.normal(k4, (E, H, D), dtype=jnp.float32) * scale}
    _L0_ffn_in = _L0_ffn_setup()
    _d = {'L0_attn_x': _L0_attn_in['x'], 'L0_attn_W_qkv': _L0_attn_in['W_qkv'], 'L0_attn_W_out': _L0_attn_in['W_out'], 'L0_attn_b_out': _L0_attn_in['b_out'], 'L0_ffn_router_w': _L0_ffn_in['router_w'], 'L0_ffn_gate_w': _L0_ffn_in['gate_w'], 'L0_ffn_up_w': _L0_ffn_in['up_w'], 'L0_ffn_down_w': _L0_ffn_in['down_w']}
    _x0 = _d['L0_attn_x']
    _d['L0_attn_x'] = jax.random.normal(jax.random.fold_in(jax.random.key(seed), 1), (16, 256, 128), dtype=_x0.dtype)
    del _x0
    return _d

def reference(L0_attn_x, L0_attn_W_qkv, L0_attn_W_out, L0_attn_b_out, L0_ffn_router_w, L0_ffn_gate_w, L0_ffn_up_w, L0_ffn_down_w):

    def _L0_attn_ref(x, W_qkv, W_out, b_out):
        import jax, jax.numpy as jnp
        import numpy as np
        DIM = 128
        B, N = (8, 512)
        EPS = 1e-06
        qkv = jnp.einsum('bnd,ed->bne', x, W_qkv)
        q, k, v = jnp.split(qkv, 3, axis=-1)
        q = jax.nn.relu(q) + EPS
        k = jax.nn.relu(k) + EPS
        kv = jnp.einsum('bnd,bne->bde', k, v)
        z = 1.0 / (jnp.einsum('bnd,bd->bn', q, k.sum(axis=1)) + EPS)
        attn = jnp.einsum('bnd,bde,bn->bne', q, kv, z)
        return jnp.einsum('bne,fe->bnf', attn, W_out) + b_out

    def _L0_ffn_ref(x, router_w, gate_w, up_w, down_w):
        import math
        import jax, jax.numpy as jnp
        from jax import lax
        import numpy as np
        E = 16
        K = 2
        CF = 1.25
        B, S, D = x.shape
        xf = x.reshape(-1, D)
        T = B * S
        capacity = max(1, math.ceil(T * K / E * CF))
        Cbuf = K * capacity
        logits = xf @ router_w
        probs = jax.nn.softmax(logits, axis=-1)
        w, idx = lax.top_k(probs, K)
        oh = jax.nn.one_hot(idx, E, dtype=w.dtype)
        rank = jnp.cumsum(oh, axis=0) - oh
        myrank = jnp.sum(rank * oh, axis=-1)
        keep = myrank < capacity
        w = jnp.where(keep, w, 0.0)
        flat_e = idx.reshape(-1)
        flat_w = w.reshape(-1)
        keep_f = keep.reshape(-1)
        tok = jnp.repeat(jnp.arange(T, dtype=jnp.int32), K)
        ohk = jax.nn.one_hot(flat_e, E, dtype=jnp.int32) * keep_f[:, None].astype(jnp.int32)
        pos = jnp.cumsum(ohk, axis=0) - ohk
        slot = jnp.sum(pos * ohk, axis=-1)
        e_idx = jnp.where(keep_f, flat_e, E)
        dispatch = jnp.full((E + 1, Cbuf), T, dtype=jnp.int32).at[e_idx, slot].set(tok)
        wbuf = jnp.zeros((E + 1, Cbuf), dtype=w.dtype).at[e_idx, slot].set(flat_w)
        dispatch = dispatch[:E]
        wbuf = wbuf[:E]
        x_pad = jnp.concatenate([xf, jnp.zeros((1, D), xf.dtype)], axis=0)
        xe = x_pad[dispatch]
        gate = jnp.einsum('ecd,edh->ech', xe, gate_w)
        up = jnp.einsum('ecd,edh->ech', xe, up_w)
        hidden = jax.nn.silu(gate) * up
        out = jnp.einsum('ech,ehd->ecd', hidden, down_w)
        out = out * wbuf[:, :, None]
        combined = jnp.zeros((T + 1, D), dtype=xf.dtype).at[dispatch.reshape(-1)].add(out.reshape(-1, D))
        return combined[:T].reshape(B, S, D)
    x = L0_attn_x
    x = x + _L0_attn_ref(_layernorm(x, axis=-1), L0_attn_W_qkv, L0_attn_W_out, L0_attn_b_out)
    x = x + _L0_ffn_ref(_layernorm(x, axis=-1), L0_ffn_router_w, L0_ffn_gate_w, L0_ffn_up_w, L0_ffn_down_w)
    return x

_drawn_inputs = setup_inputs


def setup_inputs(seed=0):
    import zlib

    import numpy as np

    out = dict(_drawn_inputs(seed))
    spreads = {}
    factors = {'L0_ffn_router_w': 8.0, 'L0_ffn_gate_w': 8.0, 'L0_ffn_up_w': 8.0, 'L0_ffn_down_w': 8.0}
    for name, (base, spread) in spreads.items():
        noise = np.random.default_rng([zlib.crc32(name.encode()), seed]).standard_normal(out[name].shape)
        drawn = base * np.exp(spread * noise) if base else spread * noise
        out[name] = jnp.asarray(drawn.astype(out[name].dtype))
    for name, factor in factors.items():
        out[name] = (out[name] * factor).astype(out[name].dtype)
    return out
```

```python
import concourse.bass as bass
from concourse import mybir
from concourse.alu_op_type import AluOpType as ALU
from contextlib import ExitStack


def linear_attention_moe(nc, x, w_qkv, w_out, b_out, router_w, gate_w, up_w, down_w,
                         xbuf, ybuf, out):
    F32, BF16 = mybir.dt.float32, mybir.dt.bfloat16
    I32, U32 = mybir.dt.int32, mybir.dt.uint32
    ACT = mybir.ActivationFunctionType
    AX = mybir.AxisListType.X

    P = 128
    NB, N, D = x.shape
    TB = N // P
    NT = NB * TB
    E = router_w.shape[1]
    K = 2
    CAP = -(-NB * N * K * 5 // (E * 4))
    BLK = 256
    A = BLK // P
    MAXB = -(-K * CAP // BLK)
    PITCH = MAXB * BLK + BLK
    SPARE = E * PITCH
    DROPPED = SPARE + BLK
    MAXN = K * NB * N // BLK + E
    MAXN += MAXN % 2
    NOROW = MAXN * BLK
    ZROW = NOROW
    ATT_EPS, LN_EPS = 1e-6, 1e-5

    with ExitStack() as ctx:
        def sb(name, shape, dt=F32):
            return ctx.enter_context(nc.sbuf_tensor(name, shape, dt))

        def sem(name):
            return ctx.enter_context(nc.semaphore(name))

        banks = [ctx.enter_context(nc.psum_tensor(f"bank{i}", [P, 512], F32)) for i in range(8)]

        wqkv_sb = sb("wqkv_sb", [P, 3, D])
        wout_sb = sb("wout_sb", [P, D])
        brow = sb("brow", [1, D])
        wqT = sb("wqT", [P, D])
        wkT = sb("wkT", [P, D])
        woT = sb("woT", [P, D])
        wvo = sb("wvo", [P, D])
        bias_bc = sb("bias_bc", [P, D])
        rw_sb = sb("rw_sb", [P, E])
        gu_sb = sb("gu_sb", [P, E + 1, 2 * D])
        dn_sb = sb("dn_sb", [P, E + 1, D])
        ident = sb("ident", [P, P])
        ones_row = sb("ones_row", [1, P])
        ones_col = sb("ones_col", [P, 1])
        ones_bf = sb("ones_bf", [P, P], BF16)
        before = sb("before", [P, P], BF16)
        tri_f = sb("tri_f", [P, P])
        minus_half = sb("minus_half", [P, TB])
        iota_i = sb("iota_i", [P, 3, E], I32)
        iota_e = sb("iota_e", [P, E])
        base_e = sb("base_e", [P, E])
        part_i = sb("part_i", [P, 1], I32)
        part = sb("part", [P, 1])
        steps_i = sb("steps_i", [P, MAXB], I32)
        steps_f = sb("steps_f", [P, MAXB])
        zeros = sb("zeros", [P, A * D])

        xs = sb("xs", [P, NT, D])
        slots = sb("slots", [P, NT * K], U32)
        yrows = sb("yrows", [P, NT * K], U32)
        oh = sb("oh", [P, NT, K, E], BF16)
        kept = sb("kept", [P, NT, K])
        wts = sb("wts", [P, NT, K])
        st1 = sb("st1", [P, 2, TB, 6])
        mv1 = sb("mv1", [P, 2, TB, 2])
        ve1 = sb("ve1", [P, 2, TB])
        rs1 = sb("rs1", [P, 2, TB])
        nb1 = sb("nb1", [P, 2, TB])
        xn = sb("xn", [P, 2, TB, D])
        xnT = sb("xnT", [P, 2, N])
        qT = sb("qT", [P, 2, N])
        kk = sb("kk", [P, 2, TB, D])
        gT = sb("gT", [P, 2, D])
        ms = sb("ms", [P, 2, D + 1])
        den = sb("den", [P, 2, TB])
        zz = sb("zz", [P, 2, TB])
        st2 = sb("st2", [P, 2, TB, 6])
        mv2 = sb("mv2", [P, 2, TB, 2])
        ve2 = sb("ve2", [P, 2, TB])
        rs2 = sb("rs2", [P, 2, TB])
        nb2 = sb("nb2", [P, 2, TB])
        xf = sb("xf", [P, 4, TB, D])
        xfT = sb("xfT", [P, 2, N])
        lmax = sb("lmax", [P, 2, TB])
        lsub = sb("lsub", [P, 2, TB, E])
        ex = sb("ex", [P, 2, TB, E])
        top = sb("top", [P, 2, TB, 8])
        tix = sb("tix", [P, 2, TB, 8], U32)
        esum = sb("esum", [P, 2, TB])
        rsum = sb("rsum", [P, 2, TB])
        wraw = sb("wraw", [P, 2, TB, K])
        seen = sb("seen", [P, 2, TB, K, E], BF16)
        p1 = sb("p1", [P, 2, TB, E])
        pos = sb("pos", [P, 2, TB, E])
        rsel = sb("rsel", [P, 2, TB, K, E])
        myrank = sb("myrank", [P, 2, TB, K])
        psel = sb("psel", [P, 2, TB, K, E])
        slot = sb("slot", [P, 2, TB, K])
        slotk = sb("slotk", [P, NT, K])

        cnt = sb("cnt", [P, E])
        cnt2 = sb("cnt2", [P, E])
        tail_f = sb("tail_f", [P, E])
        tail_i = sb("tail_i", [P, E], I32)
        more = sb("more", [P, E, MAXB])
        nblk = sb("nblk", [P, E])
        onesE = sb("onesE", [P, E])
        cum = sb("cum", [P, E])
        done = sb("done", [P, E])
        dblk = sb("dblk", [P, E])
        tab = sb("tab", [P, 2])
        first = sb("first", [P, 1])
        pairs_f = sb("pairs_f", [P, 1])
        pairs_m = sb("pairs_m", [P, 1])
        pairs_i = sb("pairs_i", [P, 1], I32)
        unused_i = sb("unused_i", [P, 1], I32)
        tabT = sb("tabT", [2, P], I32)
        row_i = sb("row_i", [1, P], I32)
        exp_i = sb("exp_i", [1, P], I32)

        cumx = sb("cumx", [P, E])
        off_e = sb("off_e", [P, E])
        osel = sb("osel", [P, NT * K, E])
        yr1 = sb("yr1", [P, NT * K])
        yr2 = sb("yr2", [P, NT * K])
        yr3 = sb("yr3", [P, NT * K])

        xe = sb("xe", [P, 2, A, D])
        xeT = sb("xeT", [P, 2, A * P])
        sg = sb("sg", [P, 2, A, D])
        hh = sb("hh", [P, 2, A, D])
        hT = sb("hT", [P, 2, A * P])
        ye = sb("ye", [P, 2, A, D])

        RING = 8
        yg = sb("yg", [P, RING, K, D])
        yo = sb("yo", [P, 4, D])
        ysum = sb("ysum", [P, 4, D])

        d_w = sem("d_w")
        d_gu, d_dn = sem("d_gu"), sem("d_dn")
        d_x = [sem(f"d_x{i}") for i in range(4)]
        d_zero = sem("d_zero")
        c_pool = sem("c_pool")
        c_dve = sem("c_dve")
        c_w = sem("c_w")
        c_wc = sem("c_wc")
        names = ("st1 mv1 nb1 rs1 ve1 xn xnT_ps xnT qk_ps qk g_ps gT ms_ps ms o_ps den zz xb att "
                 "st2 mv2 ve2 rs2 nb2 xf xfT_ps xfT lg_ps lmax lsub ex top tix esum rsum wraw oh seen0 seen "
                 "rank_ps p1 pos rsel myrank psel slot kept slotk slots").split()
        S = {n: sem("a_" + n) for n in names}
        d_sc = [sem(f"d_sc{i}") for i in range(4)]
        t_names = "cnt_ps cnt cnt2 tail more nblk cum done dblk tab first tab2 pairs pairs2 tabT_ps tabT tables rowcp cumx off osel ooff yr1 yr2 yr3 yrows".split()
        T = {n: sem("t_" + n) for n in t_names}
        d_tail = sem("d_tail")
        d_unused = sem("d_unused")
        d_tab = sem("d_tab")
        d_xe = [sem(f"d_xe{i}") for i in range(2)]
        d_ye = [sem(f"d_ye{i}") for i in range(2)]
        b_names = "xeT_ps xeT gu_ps sg hh hT_ps hT y_ps ye".split()
        B = {n: sem("b_" + n) for n in b_names}
        y_all = sem("y_all")
        d_yg = [sem(f"d_yg{i}") for i in range(RING)]
        f_sum, f_out = sem("f_sum"), sem("f_out")
        d_out = sem("d_out")

        def need(eng, s, n):
            if not (isinstance(n, int) and n <= 0):
                eng.wait_ge(s, n)

        block = ctx.enter_context(nc.Block())
        x_t = x.rearrange("b (t p) d -> p (b t) d", p=P)
        out_t = out.rearrange("b (t p) d -> p (b t) d", p=P)
        XQ = NT // 4

        A_STEPS = NB + 3

        @block.sync
        def _(sp):
            sp.dma_start(xs[:, 0:XQ, :], x_t[:, 0:XQ, :]).then_inc(d_x[0], 16)
            sp.dma_start(wqkv_sb[:, :, :], w_qkv.rearrange("(c p) d -> p c d", p=P)).then_inc(d_w, 16)
            sp.dma_start(wout_sb[:, :], w_out).then_inc(d_w, 16)
            sp.dma_start(rw_sb[:, :], router_w).then_inc(d_w, 16)
            sp.dma_start(brow[0:1, :], b_out.rearrange("(a d) -> a d", a=1)).then_inc(d_w, 16)
            for i in range(1, 4):
                sp.dma_start(xs[:, i * XQ:(i + 1) * XQ, :], x_t[:, i * XQ:(i + 1) * XQ, :]).then_inc(d_x[i], 16)
            sp.dma_start(gu_sb[:, 0:E, 0:D], gate_w.rearrange("e d h -> d e h")).then_inc(d_gu, 16)
            sp.dma_start(gu_sb[:, 0:E, D:2 * D], up_w.rearrange("e d h -> d e h")).then_inc(d_gu, 16)
            sp.dma_start(dn_sb[:, 0:E, :], down_w.rearrange("e h d -> h e d")).then_inc(d_dn, 16)
            sp.wait_ge(c_pool, 1)
            sp.dma_start(xbuf[SPARE:SPARE + BLK, :].rearrange("(p a) d -> p (a d)", a=A),
                         zeros[:, :]).then_inc(d_zero, 16)
            sp.wait_ge(T["tail"], 1)
            for i in range(4):
                sp.wait_ge(d_sc[i], 4 * NT * K)
            for e in range(0, E, 2):
                r = sp.value_load(tail_i[0:1, e:e + 1], min_val=e * PITCH, max_val=e * PITCH + K * CAP)
                sp.dma_start(xbuf[bass.ds(r, BLK), :].rearrange("(p a) d -> p (a d)", a=A),
                             zeros[:, :]).then_inc(d_tail, 16)
            sp.wait_ge(T["tables"], 2)
            pairs = sp.value_load(pairs_i[0:1, 0:1], min_val=0, max_val=MAXN // 2 - 2) + 2
            sp.wait_ge(d_zero, 16)
            sp.wait_ge(d_tail, 16 * E)

            def load(b, u, again):
                if again:
                    sp.wait_ge(B["xeT_ps"], b - 1)
                r = sp.value_load(row_i[0:1, b:b + 1] if isinstance(b, int) else row_i[0:1, bass.ds(b, 1)],
                                  min_val=0, max_val=SPARE)
                sp.dma_start(xe[:, u, :, :].rearrange("p a d -> p (a d)"),
                             xbuf[bass.ds(r, BLK), :].rearrange("(p a) d -> p (a d)", a=A)).then_inc(d_xe[u], 16)

            def store(b, u):
                sp.wait_ge(B["ye"], b + 1)
                sp.dma_start(ybuf[bass.ds(b * BLK, BLK), :].rearrange("(p a) d -> p (a d)", a=A),
                             ye[:, u, :, :].rearrange("p a d -> p (a d)")).then_inc(d_ye[u], 16)

            load(0, 0, False)
            load(1, 1, False)
            unused = sp.value_load(unused_i[0:1, 0:1], min_val=0, max_val=MAXN // 2) + 1
            with sp.Fori(0, unused) as i:
                sp.dma_start(ybuf[bass.ds(i * (-2 * BLK) + NOROW, 2 * BLK), :].rearrange("(p a) d -> p a d", a=2 * A),
                             zeros[:, 0:D].unsqueeze(1).to_broadcast([P, 2 * A, D])).then_inc(d_unused, 16)
            with sp.Fori(1, pairs) as i:
                load(2 * i, 0, True)
                store(2 * i - 2, 0)
                load(2 * i + 1, 1, True)
                store(2 * i - 1, 1)
            store(2 * pairs - 2, 0)
            store(2 * pairs - 1, 1)
            sp.wait_ge(d_ye[0], pairs * 16)
            sp.wait_ge(d_ye[1], pairs * 16)
            sp.wait_ge(d_unused, unused * 16)
            sp.sem_inc(y_all, 1)
            for g in range(NT // 4):
                sp.wait_ge(f_out, 4 * (g + 1))
                sp.dma_start(out_t[:, 4 * g:4 * g + 4, :], xs[:, 4 * g:4 * g + 4, :]).then_inc(d_out, 16)
            sp.wait_ge(d_out, 16 * (NT // 4))

        @block.gpsimd
        def _(pool):
            nc.gpsimd.memset(zeros[:, :], 0.0).then_inc(c_pool, 1)
            nc.gpsimd.memset(ident[:, :], 0.0).then_inc(c_pool, 1)
            nc.gpsimd.memset(tri_f[:, :], 1.0).then_inc(c_pool, 1)
            nc.gpsimd.memset(minus_half[:, :], -0.5).then_inc(c_pool, 1)
            nc.gpsimd.iota(iota_i[:, 0, :], pattern=[[1, E]], base=0, channel_multiplier=0).then_inc(c_pool, 1)
            nc.gpsimd.iota(iota_i[:, 1, :], pattern=[[PITCH, E]], base=0, channel_multiplier=0).then_inc(c_pool, 1)
            nc.gpsimd.iota(part_i[:, :], pattern=[[0, 1]], base=0, channel_multiplier=1).then_inc(c_pool, 1)
            nc.gpsimd.iota(steps_i[:, :], pattern=[[BLK, MAXB]], base=0, channel_multiplier=0).then_inc(c_pool, 1)
            pool.wait_ge(c_pool, 8)
            nc.gpsimd.affine_select(out=ident[:, :], in_=ident[:, :], compare_op=ALU.not_equal, fill=1.0,
                                    base=0, pattern=[[-1, P]], channel_multiplier=1).then_inc(c_pool, 1)
            nc.gpsimd.affine_select(out=tri_f[:, :], in_=tri_f[:, :], compare_op=ALU.is_gt, fill=0.0,
                                    base=0, pattern=[[1, P]], channel_multiplier=-1).then_inc(c_pool, 1)
            for s in range(NB + 4):
                if s < NB:
                    h = s % 2
                    pool.wait_ge(S["mv1"], s + 1)
                    nc.gpsimd.tensor_scalar(ve1[:, h, :], mv1[:, h, :, 1], LN_EPS, None, ALU.add).then_inc(S["ve1"], 1)
                    pool.wait_ge(S["ve1"], s + 1)
                    nc.gpsimd.tensor_tensor(rs1[:, h, :], ve1[:, h, :], minus_half[:, :], ALU.pow).then_inc(S["rs1"], 1)
                b = s - 3
                for c in range(TB * K):
                    if c == 2 and 0 <= s - 1 < NB:
                        g, h = s - 1, (s - 1) % 2
                        pool.wait_ge(S["mv2"], g + 1)
                        nc.gpsimd.tensor_scalar(ve2[:, h, :], mv2[:, h, :, 1], LN_EPS, None, ALU.add).then_inc(S["ve2"], 1)
                        pool.wait_ge(S["ve2"], g + 1)
                        nc.gpsimd.tensor_tensor(rs2[:, h, :], ve2[:, h, :], minus_half[:, :], ALU.pow).then_inc(S["rs2"], 1)
                    if 0 <= b < NB:
                        if c == 0:
                            pool.wait_ge(S["slots"], b + 1)
                        j = c // K
                        col = (TB * b + j) * K + c % K
                        nc.gpsimd.indirect_dma_start(
                            out=xbuf, out_offset=bass.IndirectOffsetOnAxis(ap=slots[:, col:col + 1], axis=0),
                            in_=xf[:, b % 4, j, :], in_offset=None,
                            bounds_check=SPARE - 1, oob_is_err=False).then_inc(d_sc[b % 4], 16)
            pool.wait_ge(T["off"], 1)
            pool.wait_ge(S["slots"], NB)
            nc.gpsimd.tensor_tensor(osel[:, :, :], oh[:, :, :, :].rearrange("p t k e -> p (t k) e"),
                                    off_e[:, :].unsqueeze(1).to_broadcast([P, NT * K, E]), ALU.mult).then_inc(T["osel"], 1)
            pool.wait_ge(T["osel"], 1)
            folds, m = 0, E // 2
            while m:
                nc.gpsimd.tensor_tensor(osel[:, :, 0:m], osel[:, :, 0:m], osel[:, :, m:2 * m],
                                        ALU.add).then_inc(T["ooff"], 1)
                folds, m = folds + 1, m // 2
                pool.wait_ge(T["ooff"], folds)
            nc.gpsimd.tensor_tensor(yr1[:, :], osel[:, :, 0], slotk[:, :, :].rearrange("p t k -> p (t k)"), ALU.add).then_inc(T["yr1"], 1)
            pool.wait_ge(T["yr1"], 1)
            nc.gpsimd.tensor_scalar(yr2[:, :], yr1[:, :], float(DROPPED - ZROW), None, ALU.add).then_inc(T["yr2"], 1)
            pool.wait_ge(T["yr2"], 1)
            nc.gpsimd.tensor_tensor(yr3[:, :], yr2[:, :], kept[:, :, :].rearrange("p t k -> p (t k)"),
                                    ALU.mult).then_inc(T["yr3"], 1)
            pool.wait_ge(T["yr3"], 1)
            nc.gpsimd.tensor_scalar(yrows[:, :], yr3[:, :], float(ZROW), None, ALU.add).then_inc(T["yrows"], 1)
            pool.wait_ge(T["yrows"], 1)
            pool.wait_ge(y_all, 1)
            for j in range(NT):
                if j >= RING:
                    pool.wait_ge(f_out, j - RING + 1)
                for k in range(K):
                    nc.gpsimd.indirect_dma_start(
                        out=yg[:, j % RING, k, :], out_offset=None, in_=ybuf,
                        in_offset=bass.IndirectOffsetOnAxis(ap=yrows[:, j * K + k:j * K + k + 1], axis=0),
                        ).then_inc(d_yg[j % RING], 16)

        @block.scalar
        def _(act):
            ORDER = []
            act.wait_ge(c_w, 1)
            nc.scalar.activation(wqT[:, :], banks[0][:, 0:D], ACT.Copy)
            nc.scalar.activation(wkT[:, :], banks[0][:, D:2 * D], ACT.Copy)
            nc.scalar.activation(woT[:, :], banks[0][:, 2 * D:3 * D], ACT.Copy)
            nc.scalar.activation(bias_bc[:, :], banks[0][:, 3 * D:4 * D], ACT.Copy).then_inc(c_wc, 1)
            act.wait_ge(c_w, 2)
            nc.scalar.activation(wvo[:, :], banks[2][:, 0:D], ACT.Copy).then_inc(c_wc, 1)

            for s in range(NB + 3):
                g, hg = s - 1, (s - 1) % 2
                if 0 <= g < NB:
                    act.wait_ge(S["ms_ps"], g + 1)
                    nc.scalar.activation(ms[:, hg, :], banks[3][:, 0:D + 1], ACT.Copy).then_inc(S["ms"], 1)
                if s < NB:
                    h = s % 2
                    act.wait_ge(S["nb1"], s + 1)
                    for j in range(TB):
                        ins = nc.scalar.activation(xn[:, h, j, :], xs[:, TB * s + j, :], ACT.Identity,
                                                   bias=nb1[:, h, j:j + 1], scale=rs1[:, h, j:j + 1])
                    ins.then_inc(S["xn"], 1)
                    act.wait_ge(S["xnT_ps"], s + 1)
                    nc.scalar.activation(xnT[:, h, :], banks[0][:, 0:N], ACT.Copy).then_inc(S["xnT"], 1)
                if 0 <= g < NB:
                    act.wait_ge(S["nb2"], g + 1)
                    if g >= 4:
                        act.wait_ge(d_sc[g % 4], 16 * TB * K * (g // 4))
                    for j in range(TB):
                        ins = nc.scalar.activation(xf[:, g % 4, j, :], xs[:, TB * g + j, :], ACT.Identity,
                                                   bias=nb2[:, hg, j:j + 1], scale=rs2[:, hg, j:j + 1])
                    ins.then_inc(S["xf"], 1)
                    act.wait_ge(S["xfT_ps"], g + 1)
                    nc.scalar.activation(xfT[:, hg, :], banks[5][:, 0:N], ACT.Copy).then_inc(S["xfT"], 1)
                    act.wait_ge(S["lsub"], g + 1)
                    nc.scalar.activation(ex[:, hg, :, :], lsub[:, hg, :, :], ACT.Exp).then_inc(S["ex"], 1)
                if s < NB:
                    act.wait_ge(S["g_ps"], s + 1)
                    nc.scalar.activation(gT[:, h, :], banks[2][:, 0:D], ACT.Copy).then_inc(S["gT"], 1)

            act.wait_ge(T["tail"], 1)
            for i in range(4):
                act.wait_ge(d_sc[i], 4 * NT * K)
            for e in range(1, E, 2):
                r = act.value_load(tail_i[0:1, e:e + 1], min_val=e * PITCH, max_val=e * PITCH + K * CAP)
                act.dma_start(xbuf[bass.ds(r, BLK), :].rearrange("(p a) d -> p (a d)", a=A),
                              zeros[:, :]).then_inc(d_tail, 16)
            act.wait_ge(T["tables"], 2)
            pairs = act.value_load(pairs_i[0:1, 0:1], min_val=0, max_val=MAXN // 2 - 2) + 2

            def xeT_copy(b, u):
                act.wait_ge(B["xeT_ps"], b + 1)
                nc.scalar.activation(xeT[:, u, :], banks[u][:, 0:A * P], ACT.Copy).then_inc(B["xeT"], 1)

            def silu(b, u):
                act.wait_ge(B["gu_ps"], b + 1)
                gate = banks[2 + u][:, :].rearrange("p (a h) -> p a h", a=A)[:, :, 0:D]
                nc.scalar.activation(sg[:, u, :, :], gate, ACT.Silu).then_inc(B["sg"], 1)

            def y_copy(b, u, again):
                act.wait_ge(B["y_ps"], b + 1)
                if again is not None:
                    act.wait_ge(d_ye[u], again)
                nc.scalar.activation(ye[:, u, :, :], banks[6 + u][:, 0:A * D].rearrange("p (a d) -> p a d", a=A),
                                     ACT.Copy).then_inc(B["ye"], 1)

            xeT_copy(0, 0)
            xeT_copy(1, 1)
            silu(0, 0)
            xeT_copy(2, 0)
            silu(1, 1)
            y_copy(0, 0, None)
            xeT_copy(3, 1)
            silu(2, 0)
            y_copy(1, 1, None)
            with act.Fori(2, pairs) as i:
                xeT_copy(2 * i, 0)
                silu(2 * i - 1, 1)
                y_copy(2 * i - 2, 0, 16 * i - 16)
                xeT_copy(2 * i + 1, 1)
                silu(2 * i, 0)
                y_copy(2 * i - 1, 1, 16 * i - 16)
            silu(2 * pairs - 1, 1)
            y_copy(2 * pairs - 2, 0, 16 * pairs - 16)
            y_copy(2 * pairs - 1, 1, 16 * pairs - 16)

        @block.vector
        def _(dve):
            dve.wait_ge(c_pool, 10)
            nc.vector.tensor_copy(before[:, :], tri_f[:, :]).then_inc(c_dve, 1)
            nc.vector.memset(ones_bf[:, :], 1.0).then_inc(c_dve, 1)
            nc.vector.memset(ones_row[:, :], 1.0).then_inc(c_dve, 1)
            nc.vector.memset(ones_col[:, :], 1.0).then_inc(c_dve, 1)
            nc.vector.tensor_copy(iota_e[:, :], iota_i[:, 0, :]).then_inc(c_dve, 1)
            nc.vector.tensor_copy(base_e[:, :], iota_i[:, 1, :]).then_inc(c_dve, 1)
            nc.vector.tensor_copy(part[:, :], part_i[:, :]).then_inc(c_dve, 1)
            nc.vector.tensor_copy(steps_f[:, :], steps_i[:, :]).then_inc(c_dve, 1)
            nc.vector.memset(seen[:, 0, 0, :, :], 0.0).then_inc(c_dve, 1)
            nc.vector.memset(gu_sb[:, E, :], 0.0).then_inc(c_dve, 1)
            nc.vector.memset(dn_sb[:, E, :], 0.0).then_inc(c_dve, 1)
            nc.vector.memset(onesE[:, :], 1.0).then_inc(c_dve, 1)
            dve.wait_ge(c_dve, 12)
            dve.wait_ge(c_wc, 1)

            def stats(st, s, h, name):
                for j in range(TB):
                    ins = nc.vector.bn_stats(st[:, h, j, :], xs[:, TB * s + j, :])
                ins.then_inc(S[name], 1)

            def aggr(mv, st, s, h, frm, name):
                dve.wait_ge(S[frm], s + 1)
                for j in range(TB):
                    ins = nc.vector.bn_aggr(mv[:, h, j, :], st[:, h, j, :])
                ins.then_inc(S[name], 1)

            def neg_bias(nb, mv, rs, s, h, frm, name):
                dve.wait_ge(S[frm], s + 1)
                nc.vector.scalar_tensor_tensor(out=nb[:, h, :], in0=mv[:, h, :, 0], scalar=-1.0, in1=rs[:, h, :],
                                               op0=ALU.mult, op1=ALU.mult).then_inc(S[name], 1)

            def top2(b, h):
                dve.wait_ge(S["ex"], b + 1)
                for j in range(TB):
                    ins = nc.vector.max(top[:, h, j, :], ex[:, h, j, :])
                ins.then_inc(S["top"], 1)
                nc.vector.reduce_sum(esum[:, h, :], ex[:, h, :, :], AX).then_inc(S["esum"], 1)
                dve.wait_ge(S["top"], b + 1)
                for j in range(TB):
                    ins = nc.vector.max_index(tix[:, h, j, :], top[:, h, j, :], ex[:, h, j, :])
                ins.then_inc(S["tix"], 1)
                dve.wait_ge(S["esum"], b + 1)
                nc.vector.reciprocal(rsum[:, h, :], esum[:, h, :]).then_inc(S["rsum"], 1)
                dve.wait_ge(S["tix"], b + 1)
                nc.vector.tensor_tensor(oh[:, TB * b:TB * b + TB, :, :],
                                        iota_e[:, :].unsqueeze(1).unsqueeze(1).to_broadcast([P, TB, K, E]),
                                        tix[:, h, :, 0:K].unsqueeze(3).to_broadcast([P, TB, K, E]),
                                        ALU.is_equal).then_inc(S["oh"], 1)
                dve.wait_ge(S["rsum"], b + 1)
                nc.vector.tensor_tensor(wraw[:, h, :, :], top[:, h, :, 0:K],
                                        rsum[:, h, :].unsqueeze(2).to_broadcast([P, TB, K]), ALU.mult).then_inc(S["wraw"], 1)
                dve.wait_ge(S["oh"], b + 1)
                need(dve, S["seen"], b)
                nc.vector.tensor_tensor(seen[:, h, 1, :, :], seen[:, h, 0, :, :], oh[:, TB * b, :, :],
                                        ALU.add).then_inc(S["seen0"], 1)
                dve.wait_ge(S["seen0"], b + 1)
                need(dve, S["rank_ps"], b)
                nc.vector.tensor_tensor(seen[:, 1 - h, 0, :, :], seen[:, h, 1, :, :], oh[:, TB * b + 1, :, :],
                                        ALU.add).then_inc(S["seen"], 1)

            def attended(b, h):
                dve.wait_ge(S["o_ps"], b + 1)
                o = banks[4][:, 0:TB * (D + 1)].rearrange("p (t d) -> p t d", t=TB)
                nc.vector.tensor_scalar(den[:, h, :], o[:, :, D], ATT_EPS, None, ALU.add).then_inc(S["den"], 1)
                dve.wait_ge(S["den"], b + 1)
                nc.vector.reciprocal(zz[:, h, :], den[:, h, :]).then_inc(S["zz"], 1)
                dve.wait_ge(S["zz"], b + 1)
                dve.wait_ge(S["xb"], b + 1)
                for j in range(TB):
                    t = TB * b + j
                    ins = nc.vector.scalar_tensor_tensor(out=xs[:, t, :], in0=o[:, j, 0:D], scalar=zz[:, h, j:j + 1],
                                                         in1=xs[:, t, :], op0=ALU.mult, op1=ALU.add)
                ins.then_inc(S["att"], 1)

            def add_bias(b):
                dve.wait_ge(S["xn"], b + 1)
                nc.vector.tensor_tensor(xs[:, TB * b:TB * b + TB, :], xs[:, TB * b:TB * b + TB, :],
                                        bias_bc[:, :].unsqueeze(1).to_broadcast([P, TB, D]), ALU.add).then_inc(S["xb"], 1)

            def place(b, h):
                dve.wait_ge(S["rank_ps"], b + 1)
                rk = banks[7][:, 0:TB * K * E].rearrange("p (t k e) -> p t k e", t=TB, k=K)
                nc.vector.tensor_tensor(rsel[:, h, :, :, :], rk, oh[:, TB * b:TB * b + TB, :, :], ALU.mult).then_inc(S["rsel"], 1)
                nc.vector.scalar_tensor_tensor(out=p1[:, h, :, :], in0=rk[:, :, 1, :], scalar=float(CAP),
                                               in1=base_e[:, :].unsqueeze(1).to_broadcast([P, TB, E]),
                                               op0=ALU.min, op1=ALU.add).then_inc(S["p1"], 1)
                dve.wait_ge(S["rsel"], b + 1)
                nc.vector.reduce_sum(myrank[:, h, :, :], rsel[:, h, :, :, :], AX).then_inc(S["myrank"], 1)
                dve.wait_ge(S["p1"], b + 1)
                nc.vector.scalar_tensor_tensor(out=pos[:, h, :, :], in0=rk[:, :, 0, :], scalar=float(CAP),
                                               in1=p1[:, h, :, :], op0=ALU.min, op1=ALU.add).then_inc(S["pos"], 1)
                dve.wait_ge(S["myrank"], b + 1)
                nc.vector.tensor_scalar(kept[:, TB * b:TB * b + TB, :], myrank[:, h, :, :], float(CAP), None,
                                        ALU.is_lt).then_inc(S["kept"], 1)
                dve.wait_ge(S["pos"], b + 1)
                nc.vector.tensor_tensor(psel[:, h, :, :, :], pos[:, h, :, :].unsqueeze(2).to_broadcast([P, TB, K, E]),
                                        oh[:, TB * b:TB * b + TB, :, :], ALU.mult).then_inc(S["psel"], 1)
                dve.wait_ge(S["kept"], b + 1)
                nc.vector.tensor_tensor(wts[:, TB * b:TB * b + TB, :], wraw[:, h, :, :], kept[:, TB * b:TB * b + TB, :], ALU.mult)
                dve.wait_ge(S["psel"], b + 1)
                nc.vector.reduce_sum(slot[:, h, :, :], psel[:, h, :, :, :], AX).then_inc(S["slot"], 1)
                dve.wait_ge(S["slot"], b + 1)
                nc.vector.scalar_tensor_tensor(out=slotk[:, TB * b:TB * b + TB, :], in0=slot[:, h, :, :], scalar=float(-DROPPED),
                                               in1=kept[:, TB * b:TB * b + TB, :], op0=ALU.add, op1=ALU.mult).then_inc(S["slotk"], 1)
                dve.wait_ge(S["slotk"], b + 1)
                nc.vector.tensor_scalar(slots[:, TB * K * b:TB * K * (b + 1)],
                                        slotk[:, TB * b:TB * b + TB, :].rearrange("p t k -> p (t k)"), float(DROPPED), None,
                                        ALU.add).then_inc(S["slots"], 1)

            def relu(b, h):
                dve.wait_ge(S["qk_ps"], b + 1)
                nc.vector.tensor_scalar(kk[:, h, :, :], banks[1][:, N:2 * N].rearrange("p (t d) -> p t d", t=TB),
                                        0.0, ATT_EPS, ALU.max, ALU.add)
                nc.vector.tensor_scalar(qT[:, h, :], banks[1][:, 0:N], 0.0, ATT_EPS, ALU.max, ALU.add).then_inc(S["qk"], 1)

            def logits_max(b, h):
                dve.wait_ge(S["lg_ps"], b + 1)
                lg = banks[6][:, 0:TB * E].rearrange("p (t e) -> p t e", t=TB)
                nc.vector.reduce_max(lmax[:, h, :], lg, AX).then_inc(S["lmax"], 1)
                dve.wait_ge(S["lmax"], b + 1)
                nc.vector.tensor_tensor(lsub[:, h, :, :], lg, lmax[:, h, :].unsqueeze(2).to_broadcast([P, TB, E]),
                                        ALU.subtract).then_inc(S["lsub"], 1)

            for s in range(NB + 3):
                h, g, hg, b, hb = s % 2, s - 1, (s - 1) % 2, s - 2, s % 2
                if s < NB:
                    if s % (NB // 4) == 0:
                        dve.wait_ge(d_x[s // (NB // 4)], 16)
                    stats(st1, s, h, "st1")
                if 0 <= b < NB:
                    top2(b, hb)
                if s < NB:
                    aggr(mv1, st1, s, h, "st1", "mv1")
                if 0 <= g < NB:
                    attended(g, hg)
                if s < NB:
                    neg_bias(nb1, mv1, rs1, s, h, "rs1", "nb1")
                if 0 <= g < NB:
                    dve.wait_ge(S["att"], g + 1)
                    stats(st2, g, hg, "st2")
                    aggr(mv2, st2, g, hg, "st2", "mv2")
                if 0 <= b < NB:
                    place(b, hb)
                if s < NB:
                    add_bias(s)
                if 0 <= g < NB:
                    neg_bias(nb2, mv2, rs2, g, hg, "rs2", "nb2")
                if s < NB:
                    relu(s, h)
                if 0 <= g < NB:
                    logits_max(g, hg)

            dve.wait_ge(T["cnt_ps"], 1)
            nc.vector.tensor_scalar(cnt[:, :], banks[7][:, 0:E], float(CAP), None, ALU.min).then_inc(T["cnt"], 1)
            dve.wait_ge(T["cnt"], 1)
            nc.vector.scalar_tensor_tensor(out=cnt2[:, :], in0=banks[7][:, E:2 * E], scalar=float(CAP), in1=cnt[:, :],
                                           op0=ALU.min, op1=ALU.add).then_inc(T["cnt2"], 1)
            dve.wait_ge(T["cnt2"], 1)
            nc.vector.tensor_tensor(tail_i[:, :], cnt2[:, :], base_e[:, :], ALU.add).then_inc(T["tail"], 1)
            nc.vector.tensor_tensor(more[:, :, :], cnt2[:, :].unsqueeze(2).to_broadcast([P, E, MAXB]),
                                    steps_f[:, :].unsqueeze(1).to_broadcast([P, E, MAXB]), ALU.is_gt).then_inc(T["more"], 1)
            dve.wait_ge(T["more"], 1)
            nc.vector.reduce_sum(nblk[:, :], more[:, :, :], AX).then_inc(T["nblk"], 1)
            dve.wait_ge(T["nblk"], 1)
            nc.vector.tensor_tensor_scan(cum[:, :], onesE[:, :], nblk[:, :], 0.0, ALU.mult, ALU.add).then_inc(T["cum"], 1)
            dve.wait_ge(T["cum"], 1)
            nc.vector.tensor_tensor(cumx[:, :], cum[:, :], nblk[:, :], ALU.subtract).then_inc(T["cumx"], 1)
            nc.vector.tensor_scalar(done[:, :], cum[:, :], part[:, 0:1], None, ALU.is_le).then_inc(T["done"], 1)
            dve.wait_ge(T["done"], 1)
            nc.vector.tensor_tensor(dblk[:, :], done[:, :], nblk[:, :], ALU.mult).then_inc(T["dblk"], 1)
            nc.vector.reduce_sum(tab[:, 0:1], done[:, :], AX).then_inc(T["tab"], 1)
            dve.wait_ge(T["dblk"], 1)
            nc.vector.reduce_sum(first[:, :], dblk[:, :], AX).then_inc(T["first"], 1)
            dve.wait_ge(T["first"], 1)
            nc.vector.tensor_tensor(pairs_f[:, :], part[:, :], first[:, :], ALU.subtract).then_inc(T["pairs"], 1)
            dve.wait_ge(T["pairs"], 1)
            dve.wait_ge(T["tab"], 1)
            nc.vector.tensor_scalar(pairs_m[:, :], pairs_f[:, :], float(BLK), None, ALU.mult).then_inc(T["pairs2"], 1)
            dve.wait_ge(T["pairs2"], 1)
            nc.vector.scalar_tensor_tensor(out=tab[:, 1:2], in0=tab[:, 0:1], scalar=float(PITCH), in1=pairs_m[:, :],
                                           op0=ALU.mult, op1=ALU.add).then_inc(T["tab2"], 1)
            nc.vector.tensor_scalar(unused_i[:, :], cum[:, E - 1:E], -0.5, MAXN // 2 - 0.25, ALU.mult, ALU.add)
            nc.vector.tensor_scalar(pairs_i[:, :], cum[:, E - 1:E], 0.5, 0.25 - 2, ALU.mult, ALU.add).then_inc(T["tables"], 1)
            dve.wait_ge(T["cumx"], 1)
            dve.wait_ge(T["tabT_ps"], 1)
            nc.vector.tensor_copy(row_i[:, :], banks[5][0:1, P:2 * P])
            nc.vector.tensor_copy(exp_i[:, :], banks[5][0:1, 0:P]).then_inc(T["tables"], 1)

            nc.vector.scalar_tensor_tensor(out=off_e[:, :], in0=cumx[:, :], scalar=float(BLK), in1=base_e[:, :],
                                           op0=ALU.mult, op1=ALU.subtract).then_inc(T["off"], 1)
            dve.wait_ge(T["tables"], 2)
            pairs = dve.value_load(pairs_i[0:1, 0:1], min_val=0, max_val=MAXN // 2 - 2) + 2

            def hidden(b, u):
                dve.wait_ge(B["sg"], b + 1)
                upv = banks[2 + u][:, :].rearrange("p (a h) -> p a h", a=A)[:, :, D:2 * D]
                nc.vector.tensor_tensor(hh[:, u, :, :], sg[:, u, :, :], upv, ALU.mult).then_inc(B["hh"], 1)

            def hT_copy(b, u):
                dve.wait_ge(B["hT_ps"], b + 1)
                nc.vector.tensor_copy(hT[:, u, :], banks[4 + u][:, 0:A * P]).then_inc(B["hT"], 1)

            hidden(0, 0)
            hT_copy(0, 0)
            hidden(1, 1)
            with dve.Fori(1, pairs) as i:
                hT_copy(2 * i - 1, 1)
                hidden(2 * i, 0)
                hT_copy(2 * i, 0)
                hidden(2 * i + 1, 1)
            hT_copy(2 * pairs - 1, 1)

            for j in range(NT):
                dve.wait_ge(d_yg[j % RING], 16 * K * (j // RING + 1))
                nc.vector.scalar_tensor_tensor(out=ysum[:, j % 4, :], in0=yg[:, j % RING, 0, :], scalar=wts[:, j, 0:1],
                                               in1=xs[:, j, :], op0=ALU.mult, op1=ALU.add).then_inc(f_sum, 1)
                dve.wait_ge(f_sum, j + 1)
                nc.vector.scalar_tensor_tensor(out=xs[:, j, :], in0=yg[:, j % RING, 1, :], scalar=wts[:, j, 1:2],
                                               in1=ysum[:, j % 4, :], op0=ALU.mult, op1=ALU.add).then_inc(f_out, 1)

        @block.tensor
        def _(pe):
            mm = nc.tensor.matmul
            pe.wait_ge(c_pool, 9)
            pe.wait_ge(c_dve, 3)
            pe.wait_ge(d_w, 64)
            nc.tensor.transpose(banks[0][:, 0:D], wqkv_sb[:, 0, :], ident[:, :])
            nc.tensor.transpose(banks[0][:, D:2 * D], wqkv_sb[:, 1, :], ident[:, :])
            nc.tensor.transpose(banks[0][:, 2 * D:3 * D], wout_sb[:, :], ident[:, :])
            mm(banks[0][:, 3 * D:4 * D], ones_row[:, :], brow[:, :], start=True, stop=True).then_inc(c_w, 1)
            pe.wait_ge(c_wc, 1)
            mm(banks[2][:, 0:D], wqkv_sb[:, 2, :], woT[:, :], start=True, stop=True).then_inc(c_w, 1)
            pe.wait_ge(c_dve, 12)
            pe.wait_ge(c_wc, 2)

            def rank_of(b, h):
                need(pe, S["slots"], b)
                pe.wait_ge(S["seen"], b + 1)
                r = banks[7][:, 0:TB * K * E]
                mm(r, before[:, :], oh[:, TB * b:TB * b + TB, :, :].rearrange("p t k e -> p (t k e)"), start=True, stop=False)
                mm(r, ones_bf[:, :], seen[:, h, :, :, :].rearrange("p t k e -> p (t k e)"), start=False, stop=True).then_inc(S["rank_ps"], 1)

            for s in range(NB + 3):
                h, g, hg, b, hb = s % 2, s - 1, (s - 1) % 2, s - 2, s % 2
                if 0 <= g < NB:
                    pe.wait_ge(S["gT"], g + 1)
                    mm(banks[3][:, 0:D], gT[:, hg, :], wvo[:, :], start=True, stop=True).then_inc(S["ms_ps"], 1)
                if 0 <= b < NB:
                    rank_of(b, hb)
                if 0 <= g < NB:
                    pe.wait_ge(S["ms"], g + 1)
                    need(pe, S["att"], g)
                    for j in range(TB):
                        ins = mm(banks[4][:, j * (D + 1):(j + 1) * (D + 1)], qT[:, hg, j * P:(j + 1) * P], ms[:, hg, :],
                                 start=True, stop=True)
                    ins.then_inc(S["o_ps"], 1)
                if s < NB:
                    pe.wait_ge(S["xn"], s + 1)
                    need(pe, S["xnT"], s)
                    for j in range(TB):
                        ins = nc.tensor.transpose(banks[0][:, j * P:(j + 1) * P], xn[:, h, j, :], ident[:, :])
                    ins.then_inc(S["xnT_ps"], 1)
                if s < NB:
                    pe.wait_ge(S["xnT"], s + 1)
                    need(pe, S["qk"], s)
                    for j in range(TB):
                        mm(banks[1][:, N + j * D:N + (j + 1) * D], xnT[:, h, j * P:(j + 1) * P], wkT[:, :], start=True, stop=True)
                    mm(banks[1][:, 0:N], wqT[:, :], xnT[:, h, :], start=True, stop=True).then_inc(S["qk_ps"], 1)
                if 0 <= g < NB:
                    pe.wait_ge(S["xf"], g + 1)
                    need(pe, S["xfT"], g)
                    for j in range(TB):
                        ins = nc.tensor.transpose(banks[5][:, j * P:(j + 1) * P], xf[:, g % 4, j, :], ident[:, :])
                    ins.then_inc(S["xfT_ps"], 1)
                if s < NB:
                    pe.wait_ge(S["qk"], s + 1)
                    need(pe, S["gT"], s)
                    for j in range(TB):
                        ins = mm(banks[2][:, 0:D], xn[:, h, j, :], kk[:, h, j, :], start=(j == 0), stop=(j == TB - 1))
                    ins.then_inc(S["g_ps"], 1)
                    need(pe, S["ms"], s)
                    for j in range(TB):
                        mm(banks[3][:, D:D + 1], kk[:, h, j, :], ones_col[:, :], start=(j == 0), stop=(j == TB - 1))
                if 0 <= g < NB:
                    pe.wait_ge(S["xfT"], g + 1)
                    need(pe, S["lsub"], g)
                    for j in range(TB):
                        ins = mm(banks[6][:, j * E:(j + 1) * E], xfT[:, hg, j * P:(j + 1) * P], rw_sb[:, :], start=True, stop=True)
                    ins.then_inc(S["lg_ps"], 1)

            pe.wait_ge(S["slots"], NB)
            pe.wait_ge(S["seen"], NB)
            mm(banks[7][:, 0:K * E], ones_bf[:, :], seen[:, NB % 2, 0, :, :].rearrange("p k e -> p (k e)"),
               start=True, stop=True).then_inc(T["cnt_ps"], 1)
            pe.wait_ge(T["tab2"], 1)
            pe.wait_ge(T["tab"], 1)
            for c in range(2):
                ins = mm(banks[5][0:1, c * P:(c + 1) * P], tab[:, c:c + 1], ident[:, :], start=True, stop=True)
            ins.then_inc(T["tabT_ps"], 1)
            pe.wait_ge(T["tables"], 2)
            pe.wait_ge(d_gu, 32)
            pe.wait_ge(d_dn, 16)
            pairs = pe.value_load(pairs_i[0:1, 0:1], min_val=0, max_val=MAXN // 2 - 2) + 2

            def expert(b):
                return pe.value_load(exp_i[0:1, bass.ds(b, 1)], min_val=0, max_val=E)

            def transpose_in(b, u, i):
                pe.wait_ge(d_xe[u], 16 * i)
                if b is not None:
                    pe.wait_ge(B["xeT"], b - 1)
                for a in range(A):
                    ins = nc.tensor.transpose(banks[u][:, a * P:(a + 1) * P], xe[:, u, a, :], ident[:, :])
                ins.then_inc(B["xeT_ps"], 1)

            def gate_up(b, u, again):
                e = expert(b)
                pe.wait_ge(B["xeT"], b + 1)
                if again:
                    pe.wait_ge(B["hh"], b - 1)
                for a in range(A):
                    ins = mm(banks[2 + u][:, a * 2 * D:(a + 1) * 2 * D], xeT[:, u, a * P:(a + 1) * P],
                             gu_sb[:, bass.ds(e, 1), :].rearrange("p o h -> p (o h)"), start=True, stop=True)
                ins.then_inc(B["gu_ps"], 1)

            def transpose_hidden(b, u, again):
                pe.wait_ge(B["hh"], b + 1)
                if again:
                    pe.wait_ge(B["hT"], b - 1)
                for a in range(A):
                    ins = nc.tensor.transpose(banks[4 + u][:, a * P:(a + 1) * P], hh[:, u, a, :], ident[:, :])
                ins.then_inc(B["hT_ps"], 1)

            def down(b, u, again):
                e = expert(b)
                pe.wait_ge(B["hT"], b + 1)
                if again:
                    pe.wait_ge(B["ye"], b - 1)
                for a in range(A):
                    ins = mm(banks[6 + u][:, a * D:(a + 1) * D], hT[:, u, a * P:(a + 1) * P],
                             dn_sb[:, bass.ds(e, 1), :].rearrange("p o d -> p (o d)"), start=True, stop=True)
                ins.then_inc(B["y_ps"], 1)

            transpose_in(None, 0, 1)
            transpose_in(None, 1, 1)
            gate_up(0, 0, False)
            transpose_in(2, 0, 2)
            transpose_hidden(0, 0, False)
            gate_up(1, 1, False)
            down(0, 0, False)
            transpose_in(3, 1, 2)
            transpose_hidden(1, 1, False)
            gate_up(2, 0, True)
            down(1, 1, False)
            with pe.Fori(2, pairs) as i:
                transpose_in(2 * i, 0, i + 1)
                transpose_hidden(2 * i - 2, 0, True)
                gate_up(2 * i - 1, 1, True)
                down(2 * i - 2, 0, True)
                transpose_in(2 * i + 1, 1, i + 1)
                transpose_hidden(2 * i - 1, 1, True)
                gate_up(2 * i, 0, True)
                down(2 * i - 1, 1, True)
            transpose_hidden(2 * pairs - 2, 0, True)
            gate_up(2 * pairs - 1, 1, True)
            down(2 * pairs - 2, 0, True)
            transpose_hidden(2 * pairs - 1, 1, True)
            down(2 * pairs - 1, 1, True)


_INS = ['L0_attn_x', 'L0_attn_W_qkv', 'L0_attn_W_out', 'L0_attn_b_out', 'L0_ffn_router_w',
        'L0_ffn_gate_w', 'L0_ffn_up_w', 'L0_ffn_down_w']


def kernel(**inputs):
    import numpy as _np
    import concourse.bacc as _bacc
    from concourse import mybir as _mybir
    from concourse.bass_utils import run_bass_kernel_spmd as _run

    nc = _bacc.Bacc("TRN2", target_bir_lowering=False, num_devices=1)
    arrays, args = {}, []
    for name in _INS:
        a = _np.ascontiguousarray(inputs[name])
        arrays[f"in_{name}_dram"] = a
        args.append(nc.dram_tensor(f"in_{name}_dram", a.shape, _mybir.dt.from_np(a.dtype), kind="ExternalInput").ap())
    f32 = _mybir.dt.float32
    D = inputs['L0_attn_x'].shape[-1]
    rows = 17 * (5 * 256 + 256)
    xbuf = nc.dram_tensor("expert_rows", (rows, D), f32).ap()
    ybuf = nc.dram_tensor("expert_results", (50 * 256, D), f32).ap()
    out = nc.dram_tensor("out_0_dram", tuple(inputs['L0_attn_x'].shape), f32, kind="ExternalOutput").ap()
    linear_attention_moe(nc, *args, xbuf, ybuf, out)
    r = _run(nc, [arrays], core_ids=[0])
    return r.results[0]["out_0_dram"]
```

```python
import concourse.bass as bass
from concourse import mybir
from concourse.alu_op_type import AluOpType as ALU
from contextlib import ExitStack


def linear_attention_moe(nc, x, w_qkv, w_out, b_out, router_w, gate_w, up_w, down_w,
                         xbuf, y2, out):
    F32, BF16 = mybir.dt.float32, mybir.dt.bfloat16
    I32, U32 = mybir.dt.int32, mybir.dt.uint32
    ACT = mybir.ActivationFunctionType
    AX = mybir.AxisListType.X

    P = 128
    NB, N, D = x.shape
    TB = N // P
    NT = NB * TB
    E = router_w.shape[1]
    K = 2
    CAP = -(-NB * N * K * 5 // (E * 4))
    BLK = 256
    A = BLK // P
    MAXB = -(-K * CAP // BLK)
    PITCH = MAXB * BLK + BLK
    SPARE = E * PITCH
    U = 4
    MINTURNS = 3
    SPARES = MINTURNS * U - CAP * K // BLK
    DROPPED = SPARE + SPARES * BLK
    MAXN = K * NB * N // BLK + E
    MAXN += -MAXN % U
    NTOK = NB * N
    W = D + 4
    FIRST, TOKEN = D, D + 1
    ATT_EPS, LN_EPS = 1e-6, 1e-5

    with ExitStack() as ctx:
        def sb(name, shape, dt=F32):
            return ctx.enter_context(nc.sbuf_tensor(name, shape, dt))

        def sem(name):
            return ctx.enter_context(nc.semaphore(name))

        banks = [ctx.enter_context(nc.psum_tensor(f"bank{i}", [P, 512], F32)) for i in range(8)]

        wqkv_sb = sb("wqkv_sb", [P, 3, D])
        wout_sb = sb("wout_sb", [P, D])
        brow = sb("brow", [1, D])
        wqT = sb("wqT", [P, D])
        wkT = sb("wkT", [P, D])
        woT = sb("woT", [P, D])
        wvo = sb("wvo", [P, D])
        bias_bc = sb("bias_bc", [P, D])
        rw_sb = sb("rw_sb", [P, E])
        gu_sb = sb("gu_sb", [P, E + 1, 2 * D])
        dn_sb = sb("dn_sb", [P, E + 1, D])
        ident = sb("ident", [P, P])
        ones_row = sb("ones_row", [1, P])
        ones_col = sb("ones_col", [P, 1])
        ones_bf = sb("ones_bf", [P, P], BF16)
        before = sb("before", [P, P], BF16)
        tri_f = sb("tri_f", [P, P])
        minus_half = sb("minus_half", [P, TB])
        tok_i = sb("tok_i", [P, NT], I32)
        tok_f = sb("tok_f", [P, NT])
        blk_i = sb("blk_i", [P, MAXN], I32)
        blk_f = sb("blk_f", [P, MAXN])
        blkrow_f = sb("blkrow_f", [P, MAXN])
        iota_i = sb("iota_i", [P, 3, E], I32)
        iota_e = sb("iota_e", [P, E])
        base_e = sb("base_e", [P, E])
        steps_i = sb("steps_i", [P, MAXB], I32)
        steps_f = sb("steps_f", [P, MAXB])
        zeros = sb("zeros", [P, D])
        tailrows = sb("tailrows", [P, A, W])

        xs = sb("xs", [P, NT, D])
        slots = sb("slots", [P, NT * K], U32)
        oh = sb("oh", [P, NT, K, E], BF16)
        kept = sb("kept", [P, NT, K])
        wts = sb("wts", [P, NT, K])
        st1 = sb("st1", [P, 2, TB, 6])
        mv1 = sb("mv1", [P, 2, TB, 2])
        ve1 = sb("ve1", [P, 2, TB])
        rs1 = sb("rs1", [P, 2, TB])
        nb1 = sb("nb1", [P, 2, TB])
        xn = sb("xn", [P, 2, TB, D])
        xnT = sb("xnT", [P, 2, N])
        qT = sb("qT", [P, 2, N])
        kk = sb("kk", [P, 2, TB, D])
        gT = sb("gT", [P, 2, D])
        ms = sb("ms", [P, 2, D + 1])
        den = sb("den", [P, 2, TB])
        zz = sb("zz", [P, 2, TB])
        st2 = sb("st2", [P, 2, TB, 6])
        mv2 = sb("mv2", [P, 2, TB, 2])
        ve2 = sb("ve2", [P, 2, TB])
        rs2 = sb("rs2", [P, 2, TB])
        nb2 = sb("nb2", [P, 2, TB])
        xf = sb("xf", [P, 4, TB, W])
        xfT = sb("xfT", [P, 2, N])
        lmax = sb("lmax", [P, 2, TB])
        lsub = sb("lsub", [P, 2, TB, E])
        ex = sb("ex", [P, 2, TB, E])
        top = sb("top", [P, 2, TB, 8])
        tix = sb("tix", [P, 2, TB, 8], U32)
        esum = sb("esum", [P, 2, TB])
        rsum = sb("rsum", [P, 2, TB])
        wraw = sb("wraw", [P, 2, TB, K])
        seen = sb("seen", [P, 2, TB, K, E], BF16)
        p1 = sb("p1", [P, 2, TB, E])
        pos = sb("pos", [P, 2, TB, E])
        rsel = sb("rsel", [P, 2, TB, K, E])
        myrank = sb("myrank", [P, 2, TB, K])
        psel = sb("psel", [P, 2, TB, K, E])
        slot = sb("slot", [P, 2, TB, K])
        slotk = sb("slotk", [P, NT, K])

        cnt = sb("cnt", [P, E])
        cnt2 = sb("cnt2", [P, E])
        tail_f = sb("tail_f", [P, E])
        tail_i = sb("tail_i", [P, E], I32)
        more = sb("more", [P, E, MAXB])
        nblk = sb("nblk", [P, E])
        onesE = sb("onesE", [P, E])
        cum = sb("cum", [P, E])
        skip = sb("skip", [P, E])
        done = sb("done", [P, MAXN, E])
        skipped = sb("skipped", [P, MAXN, E])
        eblk = sb("eblk", [P, MAXN])
        skips = sb("skips", [P, MAXN])
        blocks = sb("blocks", [P, 1])
        turns_i = sb("turns_i", [P, 1], I32)
        row_i = sb("row_i", [P, MAXN], I32)
        exp_i = sb("exp_i", [P, MAXN], I32)

        xe = sb("xe", [P, U, A, W])
        guw = sb("guw", [P, 2, 2 * D])
        xeT = sb("xeT", [P, 2, A * P])
        sg = sb("sg", [P, 2, A * P])
        hT = sb("hT", [P, 2, A * P])
        ye = sb("ye", [P, U, A, D])
        second = sb("second", [P, U, A])
        dst = sb("dst", [P, U, A], U32)

        G = 4
        yg = sb("yg", [P, K, NT, D])
        ysum = sb("ysum", [P, 4, D])

        d_w = sem("d_w")
        d_gu, d_dn = sem("d_gu"), sem("d_dn")
        d_x = [sem(f"d_x{i}") for i in range(4)]
        d_zero = sem("d_zero")
        d_spare = sem("d_spare")
        c_tail = sem("c_tail")
        c_pool = sem("c_pool")
        c_dve = sem("c_dve")
        c_w = sem("c_w")
        c_wc = sem("c_wc")
        names = ("st1 mv1 nb1 rs1 ve1 xn xnT_ps xnT qk_ps qk g_ps gT ms_ps ms o_ps den zz xb att "
                 "st2 mv2 ve2 rs2 nb2 xf xfT_ps xfT lg_ps lmax lsub ex top tix esum rsum wraw oh seen0 seen "
                 "rank_ps p1 pos rsel myrank psel slot kept slotk slots tags").split()
        S = {n: sem("a_" + n) for n in names}
        d_sc = [sem(f"d_sc{i}") for i in range(4)]
        t_names = "cnt_ps cnt cnt2 tail more nblk cum skip done blocks eblk skipped skips tables"
        T = {n: sem("t_" + n) for n in t_names.split()}
        d_tail = sem("d_tail")
        d_xe = [sem(f"d_xe{i}") for i in range(U)]
        d_ye = [sem(f"d_ye{i}") for i in range(U)]
        b_names = "guw xeT_ps xeT gu_ps sg hT y_ps ye second dst seen_ye seen_gu".split()
        B = {n: sem("b_" + n) for n in b_names}
        y_all = sem("y_all")
        d_yg = [sem(f"d_yg{g}") for g in range(NT // G)]
        f_sum, f_out = sem("f_sum"), sem("f_out")
        d_out = sem("d_out")

        def need(eng, s, n):
            if not (isinstance(n, int) and n <= 0):
                eng.wait_ge(s, n)

        block = ctx.enter_context(nc.Block())
        x_t = x.rearrange("b (t p) d -> p (b t) d", p=P)
        y2_t = y2.rearrange("(t p) d -> p t d", p=P)
        out_t = out.rearrange("b (t p) d -> p (b t) d", p=P)
        XQ = NT // 4

        A_STEPS = NB + 3

        def write_tails(eng, half):
            eng.wait_ge(T["tail"], 1)
            for e in range(half, E, 2):
                r = eng.value_load(tail_i[0:1, e:e + 1], min_val=e * PITCH, max_val=e * PITCH + K * CAP)
                eng.dma_start(xbuf[bass.ds(r, BLK), :].rearrange("(p a) w -> p a w", a=A),
                              tailrows[:, :, :]).then_inc(d_tail, 16)

        @block.sync
        def _(sp):
            sp.dma_start(xs[:, 0:XQ, :], x_t[:, 0:XQ, :]).then_inc(d_x[0], 16)
            sp.dma_start(wqkv_sb[:, :, :], w_qkv.rearrange("(c p) d -> p c d", p=P)).then_inc(d_w, 16)
            sp.dma_start(wout_sb[:, :], w_out).then_inc(d_w, 16)
            sp.dma_start(rw_sb[:, :], router_w).then_inc(d_w, 16)
            sp.dma_start(brow[0:1, :], b_out.rearrange("(a d) -> a d", a=1)).then_inc(d_w, 16)
            for i in range(1, 4):
                sp.dma_start(xs[:, i * XQ:(i + 1) * XQ, :], x_t[:, i * XQ:(i + 1) * XQ, :]).then_inc(d_x[i], 16)
            sp.dma_start(gu_sb[:, 0:E, 0:D], gate_w.rearrange("e d h -> d e h")).then_inc(d_gu, 16)
            sp.dma_start(gu_sb[:, 0:E, D:2 * D], up_w.rearrange("e d h -> d e h")).then_inc(d_gu, 16)
            sp.dma_start(dn_sb[:, 0:E, :], down_w.rearrange("e h d -> h e d")).then_inc(d_dn, 16)
            sp.wait_ge(c_pool, 2)
            sp.wait_ge(c_tail, 2)
            for i in range(SPARES):
                sp.dma_start(xbuf[SPARE + i * BLK:SPARE + (i + 1) * BLK, :].rearrange("(p a) w -> p a w", a=A),
                             tailrows[:, :, :]).then_inc(d_spare, 16)
            sp.dma_start(y2.rearrange("(p r) d -> p r d", p=P),
                         zeros[:, :].unsqueeze(1).to_broadcast([P, K * NTOK // P, D])).then_inc(d_zero, 16)
            write_tails(sp, 0)
            sp.wait_ge(T["tables"], 1)
            turns = sp.value_load(turns_i[0:1, 0:1], min_val=0, max_val=MAXN // U - MINTURNS) + MINTURNS
            sp.wait_ge(d_spare, 16 * SPARES)
            sp.wait_ge(d_tail, 16 * E)
            for i in range(4):
                sp.wait_ge(d_sc[i], 4 * NT * K)

            def load(b, u, again):
                if again:
                    sp.wait_ge(B["xeT_ps"], b - U + 1)
                    sp.wait_ge(B["dst"], b - U + 1)
                    r = sp.value_load(row_i[0:1, bass.ds(b, 1)], min_val=0, max_val=DROPPED - BLK)
                else:
                    r = sp.value_load(row_i[0:1, b:b + 1], min_val=0, max_val=DROPPED - BLK)
                sp.dma_start(xe[:, u, :, :].rearrange("p a w -> p (a w)"),
                             xbuf[bass.ds(r, BLK), :].rearrange("(p a) w -> p (a w)", a=A)).then_inc(d_xe[u], 16)

            for u in range(U):
                load(u, u, False)
            with sp.Fori(1, turns) as i:
                for u in range(U):
                    load(U * i + u, u, True)
            sp.wait_ge(y_all, 1)
            for g in range(NT // G):
                sp.dma_start(yg[:, 0, G * g:G * g + G, :], y2_t[:, G * g:G * g + G, :]).then_inc(d_yg[g], 16)
            for g in range(NT // G):
                sp.wait_ge(f_out, G * (g + 1))
                sp.dma_start(out_t[:, G * g:G * g + G, :], xs[:, G * g:G * g + G, :]).then_inc(d_out, 16)
            sp.wait_ge(d_out, 16 * (NT // G))

        @block.gpsimd
        def _(pool):
            nc.gpsimd.memset(zeros[:, :], 0.0).then_inc(c_pool, 1)
            nc.gpsimd.memset(tailrows[:, :, :], 0.0).then_inc(c_pool, 1)
            nc.gpsimd.memset(ident[:, :], 0.0).then_inc(c_pool, 1)
            nc.gpsimd.memset(tri_f[:, :], 1.0).then_inc(c_pool, 1)
            nc.gpsimd.memset(minus_half[:, :], -0.5).then_inc(c_pool, 1)
            nc.gpsimd.iota(iota_i[:, 0, :], pattern=[[1, E]], base=0, channel_multiplier=0).then_inc(c_pool, 1)
            nc.gpsimd.iota(iota_i[:, 1, :], pattern=[[PITCH, E]], base=0, channel_multiplier=0).then_inc(c_pool, 1)
            nc.gpsimd.iota(tok_i[:, :], pattern=[[P, NT]], base=0, channel_multiplier=1).then_inc(c_pool, 1)
            nc.gpsimd.iota(blk_i[:, :], pattern=[[1, MAXN]], base=0, channel_multiplier=0).then_inc(c_pool, 1)
            nc.gpsimd.iota(steps_i[:, :], pattern=[[BLK, MAXB]], base=0, channel_multiplier=0).then_inc(c_pool, 1)
            pool.wait_ge(c_pool, 10)
            nc.gpsimd.memset(tailrows[:, :, FIRST:FIRST + 1], -1.0).then_inc(c_tail, 1)
            nc.gpsimd.memset(tailrows[:, :, TOKEN:TOKEN + 1], float(K * NTOK)).then_inc(c_tail, 1)
            nc.gpsimd.affine_select(out=ident[:, :], in_=ident[:, :], compare_op=ALU.not_equal, fill=1.0,
                                    base=0, pattern=[[-1, P]], channel_multiplier=1).then_inc(c_pool, 1)
            nc.gpsimd.affine_select(out=tri_f[:, :], in_=tri_f[:, :], compare_op=ALU.is_gt, fill=0.0,
                                    base=0, pattern=[[1, P]], channel_multiplier=-1).then_inc(c_pool, 1)
            for s in range(NB + 4):
                if s < NB:
                    h = s % 2
                    pool.wait_ge(S["mv1"], s + 1)
                    nc.gpsimd.tensor_scalar(ve1[:, h, :], mv1[:, h, :, 1], LN_EPS, None, ALU.add).then_inc(S["ve1"], 1)
                    pool.wait_ge(S["ve1"], s + 1)
                    nc.gpsimd.tensor_tensor(rs1[:, h, :], ve1[:, h, :], minus_half[:, :], ALU.pow).then_inc(S["rs1"], 1)
                b = s - 3
                for c in range(TB * K):
                    if c == 2 and 0 <= s - 1 < NB:
                        g, h = s - 1, (s - 1) % 2
                        pool.wait_ge(S["mv2"], g + 1)
                        nc.gpsimd.tensor_scalar(ve2[:, h, :], mv2[:, h, :, 1], LN_EPS, None, ALU.add).then_inc(S["ve2"], 1)
                        pool.wait_ge(S["ve2"], g + 1)
                        nc.gpsimd.tensor_tensor(rs2[:, h, :], ve2[:, h, :], minus_half[:, :], ALU.pow).then_inc(S["rs2"], 1)
                    if 0 <= b < NB:
                        if c == 0:
                            pool.wait_ge(S["slots"], b + 1)
                            pool.wait_ge(S["tags"], b + 1)
                        j = c // K
                        col = (TB * b + j) * K + c % K
                        nc.gpsimd.indirect_dma_start(
                            out=xbuf, out_offset=bass.IndirectOffsetOnAxis(ap=slots[:, col:col + 1], axis=0),
                            in_=xf[:, b % 4, j, :], in_offset=None,
                            bounds_check=SPARE - 1, oob_is_err=False).then_inc(d_sc[b % 4], 16)
            pool.wait_ge(T["tables"], 1)
            turns = pool.value_load(turns_i[0:1, 0:1], min_val=0, max_val=MAXN // U - MINTURNS) + MINTURNS
            pool.wait_ge(d_zero, 16)

            def scatter(b, u):
                pool.wait_ge(B["dst"], b + 1)
                pool.sem_inc(B["seen_ye"], 1)
                pool.wait_ge(B["ye"], b + 1)
                pool.sem_inc(B["seen_ye"], 1)
                for a in range(A):
                    nc.gpsimd.indirect_dma_start(
                        out=y2, out_offset=bass.IndirectOffsetOnAxis(ap=dst[:, u, a:a + 1], axis=0),
                        in_=ye[:, u, a, :], in_offset=None,
                        bounds_check=K * NTOK - 1, oob_is_err=False).then_inc(d_ye[u], 16)

            with pool.Fori(0, turns) as i:
                for u in range(U):
                    scatter(U * i + u, u)
            for u in range(U):
                pool.wait_ge(d_ye[u], 16 * A * turns)
                pool.sem_inc(B["seen_ye"], 1)
            pool.sem_inc(y_all, 1)

        @block.scalar
        def _(act):
            ORDER = []
            act.wait_ge(c_w, 1)
            nc.scalar.activation(wqT[:, :], banks[0][:, 0:D], ACT.Copy)
            nc.scalar.activation(wkT[:, :], banks[0][:, D:2 * D], ACT.Copy)
            nc.scalar.activation(woT[:, :], banks[0][:, 2 * D:3 * D], ACT.Copy)
            nc.scalar.activation(bias_bc[:, :], banks[0][:, 3 * D:4 * D], ACT.Copy).then_inc(c_wc, 1)
            act.wait_ge(c_w, 2)
            nc.scalar.activation(wvo[:, :], banks[2][:, 0:D], ACT.Copy).then_inc(c_wc, 1)

            for s in range(NB + 3):
                g, hg = s - 1, (s - 1) % 2
                if 0 <= g < NB:
                    act.wait_ge(S["ms_ps"], g + 1)
                    nc.scalar.activation(ms[:, hg, :], banks[3][:, 0:D + 1], ACT.Copy).then_inc(S["ms"], 1)
                if s < NB:
                    h = s % 2
                    act.wait_ge(S["nb1"], s + 1)
                    for j in range(TB):
                        ins = nc.scalar.activation(xn[:, h, j, :], xs[:, TB * s + j, :], ACT.Identity,
                                                   bias=nb1[:, h, j:j + 1], scale=rs1[:, h, j:j + 1])
                    ins.then_inc(S["xn"], 1)
                    act.wait_ge(S["xnT_ps"], s + 1)
                    nc.scalar.activation(xnT[:, h, :], banks[0][:, 0:N], ACT.Copy).then_inc(S["xnT"], 1)
                b = s - 2
                if 0 <= b < NB:
                    act.wait_ge(S["tix"], b + 1)
                    nc.scalar.activation(xf[:, b % 4, :, FIRST], tix[:, b % 2, :, 0], ACT.Copy)
                    nc.scalar.activation(xf[:, b % 4, :, TOKEN], tok_f[:, TB * b:TB * b + TB], ACT.Copy).then_inc(S["tags"], 1)
                if 0 <= g < NB:
                    act.wait_ge(S["nb2"], g + 1)
                    if g >= 4:
                        act.wait_ge(d_sc[g % 4], 16 * TB * K * (g // 4))
                    for j in range(TB):
                        ins = nc.scalar.activation(xf[:, g % 4, j, 0:D], xs[:, TB * g + j, :], ACT.Identity,
                                                   bias=nb2[:, hg, j:j + 1], scale=rs2[:, hg, j:j + 1])
                    ins.then_inc(S["xf"], 1)
                    act.wait_ge(S["xfT_ps"], g + 1)
                    nc.scalar.activation(xfT[:, hg, :], banks[5][:, 0:N], ACT.Copy).then_inc(S["xfT"], 1)
                    act.wait_ge(S["lsub"], g + 1)
                    nc.scalar.activation(ex[:, hg, :, :], lsub[:, hg, :, :], ACT.Exp).then_inc(S["ex"], 1)
                if s < NB:
                    act.wait_ge(S["g_ps"], s + 1)
                    nc.scalar.activation(gT[:, h, :], banks[2][:, 0:D], ACT.Copy).then_inc(S["gT"], 1)

            write_tails(act, 1)
            act.wait_ge(T["tables"], 1)
            turns = act.value_load(turns_i[0:1, 0:1], min_val=0, max_val=MAXN // U - MINTURNS) + MINTURNS

            def xeT_copy(b, u):
                act.wait_ge(B["xeT_ps"], b + 1)
                nc.scalar.activation(xeT[:, u % 2, :], banks[u % 2][:, 0:A * P], ACT.Copy).then_inc(B["xeT"], 1)

            def silu(b, u):
                act.wait_ge(B["gu_ps"], b + 1)
                nc.scalar.activation(sg[:, u % 2, :], banks[2 + u % 2][:, 0:A * P], ACT.Silu).then_inc(B["sg"], 1)

            def y_copy(b, u, turn):
                act.wait_ge(B["y_ps"], b + 1)
                if turn is not None:
                    act.wait_ge(d_ye[u], 16 * A * turn)
                nc.scalar.activation(ye[:, u, :, :], banks[4 + u % 2][:, 0:A * D].rearrange("p (a d) -> p a d", a=A),
                                     ACT.Copy).then_inc(B["ye"], 1)

            xeT_copy(0, 0)
            xeT_copy(1, 1)
            silu(0, 0)
            xeT_copy(2, 2)
            silu(1, 1)
            y_copy(0, 0, None)
            xeT_copy(3, 3)
            silu(2, 2)
            y_copy(1, 1, None)
            def turn(i, first):
                for u in range(U):
                    xeT_copy(U * i + u, u)
                    silu(U * i + u - 1, (u - 1) % U)
                    y_copy(U * i + u - 2, (u - 2) % U, i if u >= 2 else None if first else i - 1)

            turn(1, True)
            with act.Fori(2, turns) as i:
                turn(i, False)
            silu(U * turns - 1, U - 1)
            y_copy(U * turns - 2, U - 2, turns - 1)
            y_copy(U * turns - 1, U - 1, turns - 1)
            act.wait_ge(y_all, 1)
            for g in range(NT // G):
                act.dma_start(yg[:, 1, G * g:G * g + G, :], y2_t[:, NT + G * g:NT + G * g + G, :]).then_inc(d_yg[g], 16)

        @block.vector
        def _(dve):
            dve.wait_ge(c_pool, 12)
            nc.vector.tensor_copy(before[:, :], tri_f[:, :]).then_inc(c_dve, 1)
            nc.vector.memset(ones_bf[:, :], 1.0).then_inc(c_dve, 1)
            nc.vector.memset(ones_row[:, :], 1.0).then_inc(c_dve, 1)
            nc.vector.memset(ones_col[:, :], 1.0).then_inc(c_dve, 1)
            nc.vector.tensor_copy(iota_e[:, :], iota_i[:, 0, :]).then_inc(c_dve, 1)
            nc.vector.tensor_copy(base_e[:, :], iota_i[:, 1, :]).then_inc(c_dve, 1)
            nc.vector.tensor_copy(tok_f[:, :], tok_i[:, :]).then_inc(c_dve, 1)
            nc.vector.tensor_copy(blk_f[:, :], blk_i[:, :]).then_inc(c_dve, 1)
            nc.vector.tensor_scalar(blkrow_f[:, :], blk_i[:, :], float(BLK), None, ALU.mult).then_inc(c_dve, 1)
            nc.vector.memset(xf[:, :, :, W - 2:W], 0.0).then_inc(c_dve, 1)
            nc.vector.tensor_copy(steps_f[:, :], steps_i[:, :]).then_inc(c_dve, 1)
            nc.vector.memset(seen[:, 0, 0, :, :], 0.0).then_inc(c_dve, 1)
            nc.vector.memset(gu_sb[:, E, :], 0.0).then_inc(c_dve, 1)
            nc.vector.memset(dn_sb[:, E, :], 0.0).then_inc(c_dve, 1)
            nc.vector.memset(onesE[:, :], 1.0).then_inc(c_dve, 1)
            dve.wait_ge(c_dve, 15)
            dve.wait_ge(c_wc, 1)

            def stats(st, s, h, name):
                for j in range(TB):
                    ins = nc.vector.bn_stats(st[:, h, j, :], xs[:, TB * s + j, :])
                ins.then_inc(S[name], 1)

            def aggr(mv, st, s, h, frm, name):
                dve.wait_ge(S[frm], s + 1)
                for j in range(TB):
                    ins = nc.vector.bn_aggr(mv[:, h, j, :], st[:, h, j, :])
                ins.then_inc(S[name], 1)

            def neg_bias(nb, mv, rs, s, h, frm, name):
                dve.wait_ge(S[frm], s + 1)
                nc.vector.scalar_tensor_tensor(out=nb[:, h, :], in0=mv[:, h, :, 0], scalar=-1.0, in1=rs[:, h, :],
                                               op0=ALU.mult, op1=ALU.mult).then_inc(S[name], 1)

            def top2(b, h):
                dve.wait_ge(S["ex"], b + 1)
                for j in range(TB):
                    ins = nc.vector.max(top[:, h, j, :], ex[:, h, j, :])
                ins.then_inc(S["top"], 1)
                nc.vector.reduce_sum(esum[:, h, :], ex[:, h, :, :], AX).then_inc(S["esum"], 1)
                dve.wait_ge(S["top"], b + 1)
                for j in range(TB):
                    ins = nc.vector.max_index(tix[:, h, j, :], top[:, h, j, :], ex[:, h, j, :])
                ins.then_inc(S["tix"], 1)
                dve.wait_ge(S["esum"], b + 1)
                nc.vector.reciprocal(rsum[:, h, :], esum[:, h, :]).then_inc(S["rsum"], 1)
                dve.wait_ge(S["tix"], b + 1)
                nc.vector.tensor_tensor(oh[:, TB * b:TB * b + TB, :, :],
                                        iota_e[:, :].unsqueeze(1).unsqueeze(1).to_broadcast([P, TB, K, E]),
                                        tix[:, h, :, 0:K].unsqueeze(3).to_broadcast([P, TB, K, E]),
                                        ALU.is_equal).then_inc(S["oh"], 1)
                dve.wait_ge(S["rsum"], b + 1)
                nc.vector.tensor_tensor(wraw[:, h, :, :], top[:, h, :, 0:K],
                                        rsum[:, h, :].unsqueeze(2).to_broadcast([P, TB, K]), ALU.mult).then_inc(S["wraw"], 1)
                dve.wait_ge(S["oh"], b + 1)
                need(dve, S["seen"], b)
                nc.vector.tensor_tensor(seen[:, h, 1, :, :], seen[:, h, 0, :, :], oh[:, TB * b, :, :],
                                        ALU.add).then_inc(S["seen0"], 1)
                dve.wait_ge(S["seen0"], b + 1)
                need(dve, S["rank_ps"], b)
                nc.vector.tensor_tensor(seen[:, 1 - h, 0, :, :], seen[:, h, 1, :, :], oh[:, TB * b + 1, :, :],
                                        ALU.add).then_inc(S["seen"], 1)

            def attended(b, h):
                dve.wait_ge(S["o_ps"], b + 1)
                o = banks[4][:, 0:TB * (D + 1)].rearrange("p (t d) -> p t d", t=TB)
                nc.vector.tensor_scalar(den[:, h, :], o[:, :, D], ATT_EPS, None, ALU.add).then_inc(S["den"], 1)
                dve.wait_ge(S["den"], b + 1)
                nc.vector.reciprocal(zz[:, h, :], den[:, h, :]).then_inc(S["zz"], 1)
                dve.wait_ge(S["zz"], b + 1)
                dve.wait_ge(S["xb"], b + 1)
                for j in range(TB):
                    t = TB * b + j
                    ins = nc.vector.scalar_tensor_tensor(out=xs[:, t, :], in0=o[:, j, 0:D], scalar=zz[:, h, j:j + 1],
                                                         in1=xs[:, t, :], op0=ALU.mult, op1=ALU.add)
                ins.then_inc(S["att"], 1)

            def add_bias(b):
                dve.wait_ge(S["xn"], b + 1)
                nc.vector.tensor_tensor(xs[:, TB * b:TB * b + TB, :], xs[:, TB * b:TB * b + TB, :],
                                        bias_bc[:, :].unsqueeze(1).to_broadcast([P, TB, D]), ALU.add).then_inc(S["xb"], 1)

            def place(b, h):
                dve.wait_ge(S["rank_ps"], b + 1)
                rk = banks[7][:, 0:TB * K * E].rearrange("p (t k e) -> p t k e", t=TB, k=K)
                nc.vector.tensor_tensor(rsel[:, h, :, :, :], rk, oh[:, TB * b:TB * b + TB, :, :], ALU.mult).then_inc(S["rsel"], 1)
                nc.vector.scalar_tensor_tensor(out=p1[:, h, :, :], in0=rk[:, :, 1, :], scalar=float(CAP),
                                               in1=base_e[:, :].unsqueeze(1).to_broadcast([P, TB, E]),
                                               op0=ALU.min, op1=ALU.add).then_inc(S["p1"], 1)
                dve.wait_ge(S["rsel"], b + 1)
                nc.vector.reduce_sum(myrank[:, h, :, :], rsel[:, h, :, :, :], AX).then_inc(S["myrank"], 1)
                dve.wait_ge(S["p1"], b + 1)
                nc.vector.scalar_tensor_tensor(out=pos[:, h, :, :], in0=rk[:, :, 0, :], scalar=float(CAP),
                                               in1=p1[:, h, :, :], op0=ALU.min, op1=ALU.add).then_inc(S["pos"], 1)
                dve.wait_ge(S["myrank"], b + 1)
                nc.vector.tensor_scalar(kept[:, TB * b:TB * b + TB, :], myrank[:, h, :, :], float(CAP), None,
                                        ALU.is_lt).then_inc(S["kept"], 1)
                dve.wait_ge(S["pos"], b + 1)
                nc.vector.tensor_tensor(psel[:, h, :, :, :], pos[:, h, :, :].unsqueeze(2).to_broadcast([P, TB, K, E]),
                                        oh[:, TB * b:TB * b + TB, :, :], ALU.mult).then_inc(S["psel"], 1)
                dve.wait_ge(S["kept"], b + 1)
                nc.vector.tensor_tensor(wts[:, TB * b:TB * b + TB, :], wraw[:, h, :, :], kept[:, TB * b:TB * b + TB, :], ALU.mult)
                dve.wait_ge(S["psel"], b + 1)
                nc.vector.reduce_sum(slot[:, h, :, :], psel[:, h, :, :, :], AX).then_inc(S["slot"], 1)
                dve.wait_ge(S["slot"], b + 1)
                nc.vector.scalar_tensor_tensor(out=slotk[:, TB * b:TB * b + TB, :], in0=slot[:, h, :, :], scalar=float(-DROPPED),
                                               in1=kept[:, TB * b:TB * b + TB, :], op0=ALU.add, op1=ALU.mult).then_inc(S["slotk"], 1)
                dve.wait_ge(S["slotk"], b + 1)
                nc.vector.tensor_scalar(slots[:, TB * K * b:TB * K * (b + 1)],
                                        slotk[:, TB * b:TB * b + TB, :].rearrange("p t k -> p (t k)"), float(DROPPED), None,
                                        ALU.add).then_inc(S["slots"], 1)

            def relu(b, h):
                dve.wait_ge(S["qk_ps"], b + 1)
                nc.vector.tensor_scalar(kk[:, h, :, :], banks[1][:, N:2 * N].rearrange("p (t d) -> p t d", t=TB),
                                        0.0, ATT_EPS, ALU.max, ALU.add)
                nc.vector.tensor_scalar(qT[:, h, :], banks[1][:, 0:N], 0.0, ATT_EPS, ALU.max, ALU.add).then_inc(S["qk"], 1)

            def logits_max(b, h):
                dve.wait_ge(S["lg_ps"], b + 1)
                lg = banks[6][:, 0:TB * E].rearrange("p (t e) -> p t e", t=TB)
                nc.vector.reduce_max(lmax[:, h, :], lg, AX).then_inc(S["lmax"], 1)
                dve.wait_ge(S["lmax"], b + 1)
                nc.vector.tensor_tensor(lsub[:, h, :, :], lg, lmax[:, h, :].unsqueeze(2).to_broadcast([P, TB, E]),
                                        ALU.subtract).then_inc(S["lsub"], 1)

            for s in range(NB + 3):
                h, g, hg, b, hb = s % 2, s - 1, (s - 1) % 2, s - 2, s % 2
                if s < NB:
                    if s % (NB // 4) == 0:
                        dve.wait_ge(d_x[s // (NB // 4)], 16)
                    stats(st1, s, h, "st1")
                if 0 <= b < NB:
                    top2(b, hb)
                if s < NB:
                    aggr(mv1, st1, s, h, "st1", "mv1")
                if 0 <= g < NB:
                    attended(g, hg)
                if s < NB:
                    neg_bias(nb1, mv1, rs1, s, h, "rs1", "nb1")
                if 0 <= g < NB:
                    dve.wait_ge(S["att"], g + 1)
                    stats(st2, g, hg, "st2")
                    aggr(mv2, st2, g, hg, "st2", "mv2")
                if 0 <= b < NB:
                    place(b, hb)
                if s < NB:
                    add_bias(s)
                if 0 <= g < NB:
                    neg_bias(nb2, mv2, rs2, g, hg, "rs2", "nb2")
                if s < NB:
                    relu(s, h)
                if 0 <= g < NB:
                    logits_max(g, hg)

            dve.wait_ge(T["cnt_ps"], 1)
            nc.vector.tensor_scalar(cnt[:, :], banks[7][:, 0:E], float(CAP), None, ALU.min).then_inc(T["cnt"], 1)
            dve.wait_ge(T["cnt"], 1)
            nc.vector.scalar_tensor_tensor(out=cnt2[:, :], in0=banks[7][:, E:2 * E], scalar=float(CAP), in1=cnt[:, :],
                                           op0=ALU.min, op1=ALU.add).then_inc(T["cnt2"], 1)
            dve.wait_ge(T["cnt2"], 1)
            nc.vector.tensor_tensor(tail_i[:, :], cnt2[:, :], base_e[:, :], ALU.add).then_inc(T["tail"], 1)
            nc.vector.tensor_tensor(more[:, :, :], cnt2[:, :].unsqueeze(2).to_broadcast([P, E, MAXB]),
                                    steps_f[:, :].unsqueeze(1).to_broadcast([P, E, MAXB]), ALU.is_gt).then_inc(T["more"], 1)
            dve.wait_ge(T["more"], 1)
            nc.vector.reduce_sum(nblk[:, :], more[:, :, :], AX).then_inc(T["nblk"], 1)
            dve.wait_ge(T["nblk"], 1)
            nc.vector.tensor_tensor_scan(cum[:, :], onesE[:, :], nblk[:, :], 0.0, ALU.mult, ALU.add).then_inc(T["cum"], 1)
            dve.wait_ge(T["cum"], 1)
            nc.vector.tensor_tensor(done[:, :, :], cum[:, :].unsqueeze(1).to_broadcast([P, MAXN, E]),
                                    blk_f[:, :].unsqueeze(2).to_broadcast([P, MAXN, E]), ALU.is_le).then_inc(T["done"], 1)
            nc.vector.tensor_scalar(skip[:, :], nblk[:, :], float(-BLK), float(PITCH), ALU.mult, ALU.add).then_inc(T["skip"], 1)
            nc.vector.tensor_scalar(blocks[:, :], cum[:, E - 1:E], float(MINTURNS * U), None, ALU.max).then_inc(T["blocks"], 1)
            dve.wait_ge(T["done"], 1)
            nc.vector.reduce_sum(eblk[:, :], done[:, :, :], AX).then_inc(T["eblk"], 1)
            dve.wait_ge(T["blocks"], 1)
            nc.vector.tensor_scalar(turns_i[:, :], blocks[:, :], 1.0 / U, 0.375 - MINTURNS, ALU.mult, ALU.add)
            dve.wait_ge(T["skip"], 1)
            nc.vector.tensor_tensor(skipped[:, :, :], done[:, :, :], skip[:, :].unsqueeze(1).to_broadcast([P, MAXN, E]),
                                    ALU.mult).then_inc(T["skipped"], 1)
            dve.wait_ge(T["skipped"], 1)
            nc.vector.reduce_sum(skips[:, :], skipped[:, :, :], AX).then_inc(T["skips"], 1)
            dve.wait_ge(T["eblk"], 1)
            nc.vector.tensor_copy(exp_i[:, :], eblk[:, :])
            dve.wait_ge(T["skips"], 1)
            nc.vector.tensor_tensor(row_i[:, :], skips[:, :], blkrow_f[:, :], ALU.add).then_inc(T["tables"], 1)
            dve.wait_ge(T["tables"], 1)
            turns = dve.value_load(turns_i[0:1, 0:1], min_val=0, max_val=MAXN // U - MINTURNS) + MINTURNS

            def weights(b, u, again):
                e = dve.value_load(exp_i[0:1, bass.ds(b, 1)] if again else exp_i[0:1, b:b + 1], min_val=0, max_val=E)
                if again or u >= 2:
                    dve.wait_ge(B["gu_ps"], b - 1)
                    if again:
                        dve.sem_inc(B["seen_gu"], 1)
                nc.vector.tensor_copy(guw[:, u % 2, :], gu_sb[:, bass.ds(e, 1), :].rearrange("p o h -> p (o h)")).then_inc(B["guw"], 1)

            def targets(b, u, turn):
                dve.wait_ge(d_xe[u], 16 * turn)
                if not isinstance(turn, int):
                    dve.sem_inc(B["seen_gu"], 1)
                nc.vector.tensor_tensor(second[:, u, :], xe[:, u, :, FIRST],
                                        (eblk[:, bass.ds(b, 1)] if not isinstance(turn, int) else eblk[:, b:b + 1]).to_broadcast([P, A]),
                                        ALU.not_equal).then_inc(B["second"], 1)
                dve.wait_ge(B["second"], b + 1)
                if not isinstance(turn, int):
                    dve.wait_ge(d_ye[u], 16 * A * (turn - 1))
                nc.vector.scalar_tensor_tensor(out=dst[:, u, :], in0=second[:, u, :], scalar=float(NTOK), in1=xe[:, u, :, TOKEN],
                                               op0=ALU.mult, op1=ALU.add).then_inc(B["dst"], 1)

            def hidden(b, u):
                dve.wait_ge(B["sg"], b + 1)
                nc.vector.tensor_tensor(hT[:, u % 2, :], sg[:, u % 2, :], banks[2 + u % 2][:, A * P:2 * A * P],
                                        ALU.mult).then_inc(B["hT"], 1)

            dve.wait_ge(d_gu, 32)
            for u in range(U):
                weights(u, u, False)
                targets(u, u, 1)
                if u:
                    hidden(u - 1, u - 1)
            with dve.Fori(1, turns) as i:
                for u in range(U):
                    weights(U * i + u, u, True)
                    targets(U * i + u, u, i + 1)
                    hidden(U * i + u - 1, (u - 1) % U)
            hidden(U * turns - 1, U - 1)

            for j in range(NT):
                if j % G == 0:
                    dve.wait_ge(d_yg[j // G], 16 * K)
                nc.vector.scalar_tensor_tensor(out=ysum[:, j % 4, :], in0=yg[:, 0, j, :], scalar=wts[:, j, 0:1],
                                               in1=xs[:, j, :], op0=ALU.mult, op1=ALU.add).then_inc(f_sum, 1)
                dve.wait_ge(f_sum, j + 1)
                nc.vector.scalar_tensor_tensor(out=xs[:, j, :], in0=yg[:, 1, j, :], scalar=wts[:, j, 1:2],
                                               in1=ysum[:, j % 4, :], op0=ALU.mult, op1=ALU.add).then_inc(f_out, 1)

        @block.tensor
        def _(pe):
            mm = nc.tensor.matmul
            pe.wait_ge(c_pool, 11)
            pe.wait_ge(c_dve, 3)
            pe.wait_ge(d_w, 64)
            nc.tensor.transpose(banks[0][:, 0:D], wqkv_sb[:, 0, :], ident[:, :])
            nc.tensor.transpose(banks[0][:, D:2 * D], wqkv_sb[:, 1, :], ident[:, :])
            nc.tensor.transpose(banks[0][:, 2 * D:3 * D], wout_sb[:, :], ident[:, :])
            mm(banks[0][:, 3 * D:4 * D], ones_row[:, :], brow[:, :], start=True, stop=True).then_inc(c_w, 1)
            pe.wait_ge(c_wc, 1)
            mm(banks[2][:, 0:D], wqkv_sb[:, 2, :], woT[:, :], start=True, stop=True).then_inc(c_w, 1)
            pe.wait_ge(c_dve, 15)
            pe.wait_ge(c_wc, 2)

            def rank_of(b, h):
                need(pe, S["slots"], b)
                pe.wait_ge(S["seen"], b + 1)
                r = banks[7][:, 0:TB * K * E]
                mm(r, before[:, :], oh[:, TB * b:TB * b + TB, :, :].rearrange("p t k e -> p (t k e)"), start=True, stop=False)
                mm(r, ones_bf[:, :], seen[:, h, :, :, :].rearrange("p t k e -> p (t k e)"), start=False, stop=True).then_inc(S["rank_ps"], 1)

            for s in range(NB + 3):
                h, g, hg, b, hb = s % 2, s - 1, (s - 1) % 2, s - 2, s % 2
                if 0 <= g < NB:
                    pe.wait_ge(S["gT"], g + 1)
                    mm(banks[3][:, 0:D], gT[:, hg, :], wvo[:, :], start=True, stop=True).then_inc(S["ms_ps"], 1)
                if 0 <= b < NB:
                    rank_of(b, hb)
                if 0 <= g < NB:
                    pe.wait_ge(S["ms"], g + 1)
                    need(pe, S["att"], g)
                    for j in range(TB):
                        ins = mm(banks[4][:, j * (D + 1):(j + 1) * (D + 1)], qT[:, hg, j * P:(j + 1) * P], ms[:, hg, :],
                                 start=True, stop=True)
                    ins.then_inc(S["o_ps"], 1)
                if s < NB:
                    pe.wait_ge(S["xn"], s + 1)
                    need(pe, S["xnT"], s)
                    for j in range(TB):
                        ins = nc.tensor.transpose(banks[0][:, j * P:(j + 1) * P], xn[:, h, j, :], ident[:, :])
                    ins.then_inc(S["xnT_ps"], 1)
                if s < NB:
                    pe.wait_ge(S["xnT"], s + 1)
                    need(pe, S["qk"], s)
                    for j in range(TB):
                        mm(banks[1][:, N + j * D:N + (j + 1) * D], xnT[:, h, j * P:(j + 1) * P], wkT[:, :], start=True, stop=True)
                    mm(banks[1][:, 0:N], wqT[:, :], xnT[:, h, :], start=True, stop=True).then_inc(S["qk_ps"], 1)
                if 0 <= g < NB:
                    pe.wait_ge(S["xf"], g + 1)
                    need(pe, S["xfT"], g)
                    for j in range(TB):
                        ins = nc.tensor.transpose(banks[5][:, j * P:(j + 1) * P], xf[:, g % 4, j, 0:D], ident[:, :])
                    ins.then_inc(S["xfT_ps"], 1)
                if s < NB:
                    pe.wait_ge(S["qk"], s + 1)
                    need(pe, S["gT"], s)
                    for j in range(TB):
                        ins = mm(banks[2][:, 0:D], xn[:, h, j, :], kk[:, h, j, :], start=(j == 0), stop=(j == TB - 1))
                    ins.then_inc(S["g_ps"], 1)
                    need(pe, S["ms"], s)
                    for j in range(TB):
                        mm(banks[3][:, D:D + 1], kk[:, h, j, :], ones_col[:, :], start=(j == 0), stop=(j == TB - 1))
                if 0 <= g < NB:
                    pe.wait_ge(S["xfT"], g + 1)
                    need(pe, S["lsub"], g)
                    for j in range(TB):
                        ins = mm(banks[6][:, j * E:(j + 1) * E], xfT[:, hg, j * P:(j + 1) * P], rw_sb[:, :], start=True, stop=True)
                    ins.then_inc(S["lg_ps"], 1)

            pe.wait_ge(S["slots"], NB)
            pe.wait_ge(S["seen"], NB)
            mm(banks[7][:, 0:K * E], ones_bf[:, :], seen[:, NB % 2, 0, :, :].rearrange("p k e -> p (k e)"),
               start=True, stop=True).then_inc(T["cnt_ps"], 1)
            pe.wait_ge(T["tables"], 1)
            pe.wait_ge(d_dn, 16)
            turns = pe.value_load(turns_i[0:1, 0:1], min_val=0, max_val=MAXN // U - MINTURNS) + MINTURNS

            def transpose_in(b, u, turn):
                pe.wait_ge(d_xe[u], 16 * turn)
                if b is not None:
                    pe.wait_ge(B["xeT"], b - 1)
                for a in range(A):
                    ins = nc.tensor.transpose(banks[u % 2][:, a * P:(a + 1) * P], xe[:, u, a, 0:D], ident[:, :])
                ins.then_inc(B["xeT_ps"], 1)

            def gate_up(b, u, again):
                pe.wait_ge(B["xeT"], b + 1)
                pe.wait_ge(B["guw"], b + 1)
                if again:
                    pe.wait_ge(B["hT"], b - 1)
                for c in range(2):
                    ins = mm(banks[2 + u % 2][:, c * A * P:(c + 1) * A * P], guw[:, u % 2, c * D:(c + 1) * D], xeT[:, u % 2, :],
                             start=True, stop=True)
                ins.then_inc(B["gu_ps"], 1)

            def down(b, u, again):
                e = pe.value_load(exp_i[0:1, b:b + 1] if isinstance(b, int) else exp_i[0:1, bass.ds(b, 1)],
                                  min_val=0, max_val=E)
                pe.wait_ge(B["hT"], b + 1)
                if again:
                    pe.wait_ge(B["ye"], b - 1)
                for a in range(A):
                    ins = mm(banks[4 + u % 2][:, a * D:(a + 1) * D], hT[:, u % 2, a * P:(a + 1) * P],
                             dn_sb[:, bass.ds(e, 1), :].rearrange("p o d -> p (o d)"), start=True, stop=True)
                ins.then_inc(B["y_ps"], 1)

            transpose_in(None, 0, 1)
            transpose_in(None, 1, 1)
            gate_up(0, 0, False)
            transpose_in(2, 2, 1)
            gate_up(1, 1, False)
            down(0, 0, False)
            transpose_in(3, 3, 1)
            gate_up(2, 2, True)
            down(1, 1, False)
            with pe.Fori(1, turns) as i:
                for u in range(U):
                    transpose_in(U * i + u, u, i + 1)
                    gate_up(U * i + u - 1, (u - 1) % U, True)
                    down(U * i + u - 2, (u - 2) % U, True)
            gate_up(U * turns - 1, U - 1, True)
            down(U * turns - 2, U - 2, True)
            down(U * turns - 1, U - 1, True)


_INS = ['L0_attn_x', 'L0_attn_W_qkv', 'L0_attn_W_out', 'L0_attn_b_out', 'L0_ffn_router_w',
        'L0_ffn_gate_w', 'L0_ffn_up_w', 'L0_ffn_down_w']


def kernel(**inputs):
    import numpy as _np
    import concourse.bacc as _bacc
    from concourse import mybir as _mybir
    from concourse.bass_utils import run_bass_kernel_spmd as _run

    nc = _bacc.Bacc("TRN2", target_bir_lowering=False, num_devices=1)
    arrays, args = {}, []
    for name in _INS:
        a = _np.ascontiguousarray(inputs[name])
        arrays[f"in_{name}_dram"] = a
        args.append(nc.dram_tensor(f"in_{name}_dram", a.shape, _mybir.dt.from_np(a.dtype), kind="ExternalInput").ap())
    f32 = _mybir.dt.float32
    D = inputs['L0_attn_x'].shape[-1]
    E, CAPK, BLK = inputs['L0_ffn_router_w'].shape[1], 1280, 256
    T = inputs['L0_attn_x'].shape[0] * inputs['L0_attn_x'].shape[1]
    rows = E * (CAPK + BLK) + 7 * BLK
    xbuf = nc.dram_tensor("expert_rows", (rows, D + 4), f32).ap()
    y2 = nc.dram_tensor("expert_results", (2 * T, D), f32).ap()
    out = nc.dram_tensor("out_0_dram", tuple(inputs['L0_attn_x'].shape), f32, kind="ExternalOutput").ap()
    linear_attention_moe(nc, *args, xbuf, y2, out)
    r = _run(nc, [arrays], core_ids=[0])
    return r.results[0]["out_0_dram"]
```

```python
import concourse.bass as bass
from concourse import mybir
from concourse.alu_op_type import AluOpType as ALU
from contextlib import ExitStack


def sizes(tokens, experts, choices):
    cap = -(-tokens * choices * 5 // (experts * 4))
    blk = 128
    maxb = -(-choices * cap // blk)
    pitch = maxb * blk + blk
    per_turn = 8
    minturns = 3
    spares = max(per_turn - 1, minturns * per_turn - choices * cap // blk)
    return cap, blk, maxb, pitch, per_turn, minturns, spares


def linear_attention_moe(nc, x, w_qkv, w_out, b_out, router_w, gate_w, up_w, down_w,
                         xbuf, y2, out):
    F32, BF16 = mybir.dt.float32, mybir.dt.bfloat16
    I32, U32 = mybir.dt.int32, mybir.dt.uint32
    ACT = mybir.ActivationFunctionType
    AX = mybir.AxisListType.X

    P = 128
    NB, N, D = x.shape
    TB = N // P
    NT = NB * TB
    E = router_w.shape[1]
    K = 2
    CAP, BLK, MAXB, PITCH, U, MINTURNS, SPARES = sizes(NB * N, E, K)
    SPARE = E * PITCH
    DROPPED = SPARE + SPARES * BLK
    MAXN = K * NB * N // BLK + E
    MAXN += -MAXN % U
    NTOK = NB * N
    W = D + 4
    FIRST, TOKEN = D, D + 1
    R = 6
    FIRSTS = tuple(range(0, NB + 1, 2))
    ATT_EPS, LN_EPS = 1e-6, 1e-5
    WAKE = 10

    with ExitStack() as ctx:
        def sb(name, shape, dt=F32):
            return ctx.enter_context(nc.sbuf_tensor(name, shape, dt))

        def sem(name):
            return ctx.enter_context(nc.semaphore(name))

        banks = [ctx.enter_context(nc.psum_tensor(f"bank{i}", [P, 512], F32)) for i in range(8)]

        wqkv_sb = sb("wqkv_sb", [P, 3, D])
        wout_sb = sb("wout_sb", [P, D])
        brow = sb("brow", [1, D])
        wqT = sb("wqT", [P, D])
        wkT = sb("wkT", [P, D])
        woT = sb("woT", [P, D])
        wvo = sb("wvo", [P, D])
        bias_bc = sb("bias_bc", [P, D])
        rw_sb = sb("rw_sb", [P, E])
        ew_sb = sb("ew_sb", [P, E + 1, 3 * D])
        ident = sb("ident", [P, P])
        ones_row = sb("ones_row", [1, P])
        ones_col = sb("ones_col", [P, 1])
        ones_bf = sb("ones_bf", [P, P], BF16)
        before = sb("before", [P, P], BF16)
        tri_f = sb("tri_f", [P, P])
        warm = sb("warm", [P, 1])
        eps_col = sb("eps_col", [P, 1])
        tok_i = sb("tok_i", [P, NT], I32)
        tok_f = sb("tok_f", [P, NT])
        part_i = sb("part_i", [P, 1], I32)
        part = sb("part", [P, 1])
        partrow = sb("partrow", [P, 1])
        iota_i = sb("iota_i", [P, 3, E], I32)
        iota_e = sb("iota_e", [P, E])
        base_e = sb("base_e", [P, E])
        steps_i = sb("steps_i", [P, MAXB], I32)
        steps_f = sb("steps_f", [P, MAXB])
        zeros = sb("zeros", [P, D])
        tailrows = sb("tailrows", [P, W])

        xs = sb("xs", [P, NT, D])
        xa = sb("xa", [P, NT, D])
        slots = sb("slots", [P, NT * K], U32)
        oh = sb("oh", [P, NT, K, E], BF16)
        kept = sb("kept", [P, NT, K])
        wts = sb("wts", [P, NT, K])
        st1 = sb("st1", [P, NT, 6])
        st2 = sb("st2", [P, R, TB, 6])
        mv1 = sb("mv1", [P, NT, 2])
        rs1 = sb("rs1", [P, NT])
        nb1 = sb("nb1", [P, NT])
        ve1 = sb("ve1", [P, NT])
        mv2 = sb("mv2", [P, R, TB, 2])
        rs2 = sb("rs2", [P, R * TB])
        nb2 = sb("nb2", [P, R * TB])
        ve2 = sb("ve2", [P, R * TB])
        minus_half = sb("minus_half", [P, NT])
        xn = sb("xn", [P, R, TB, D])
        xnT = sb("xnT", [P, R, N])
        qk = sb("qk", [P, R, 2 * N])
        gs = sb("gs", [P, R, 2 * D + 1])
        den = sb("den", [P, R, TB])
        zz = sb("zz", [P, R, TB])
        xf = sb("xf", [P, R, TB, W])
        xfT = sb("xfT", [P, R, N])
        lmax = sb("lmax", [P, R, TB])
        lsub = sb("lsub", [P, R, TB, E])
        ex = sb("ex", [P, R, TB, E])
        top = sb("top", [P, R, TB, 8])
        tix = sb("tix", [P, R, TB, 8], U32)
        esum = sb("esum", [P, R, TB])
        rsum = sb("rsum", [P, R, TB])
        wraw = sb("wraw", [P, R, TB, K])
        seen = sb("seen", [P, R, TB, K, E], BF16)
        p1 = sb("p1", [P, R, TB, E])
        pos = sb("pos", [P, R, TB, E])
        sel = sb("sel", [P, R, 2, TB, K, E])
        rank_slot = sb("rank_slot", [P, R, 2, TB, K])
        slotk = sb("slotk", [P, R, TB, K])

        cnt = sb("cnt", [P, E])
        cnt2 = sb("cnt2", [P, E])
        tail_i = sb("tail_i", [P, E], I32)
        more = sb("more", [P, E, MAXB])
        nblk = sb("nblk", [P, E])
        onesE = sb("onesE", [P, E])
        cum = sb("cum", [P, E])
        skip = sb("skip", [P, E])
        done = sb("done", [P, 2, E])
        table = sb("table", [P, 2])
        table2 = sb("table2", [P, 1])
        blocks = sb("blocks", [P, 1])
        turns_i = sb("turns_i", [P, 1], I32)
        row_i = sb("row_i", [1, P], I32)
        exp_i = sb("exp_i", [1, P], I32)
        eblk = sb("eblk", [P, P])
        eturn = sb("eturn", [P, U])

        xe = sb("xe", [P, U, W])
        ew = sb("ew", [P, U, 3 * D])
        xeT = sb("xeT", [P, 2, P])
        sg = sb("sg", [P, 2, P])
        hT = sb("hT", [P, 2, P])
        ye = sb("ye", [P, U, D])
        second = sb("second", [P, U])
        dst = sb("dst", [P, U], U32)

        G = 4
        yg = sb("yg", [P, K, NT, D])
        ysum = sb("ysum", [P, NT, D])

        d_w = sem("d_w")
        d_ew = sem("d_ew")
        d_x = [sem(f"d_x{i}") for i in range(4)]
        d_zero = sem("d_zero")
        d_spare = sem("d_spare")
        c_tail = sem("c_tail")
        c_pool = sem("c_pool")
        c_dve = sem("c_dve")
        c_w = sem("c_w")
        c_wc = sem("c_wc")
        names = ("st1 ag1 nb1 ve1 rs1 ve2 rs2 nb2 xn T cT QK qr qk G gT M ms O den zz xb x1 st2 ag2 xf T2 cT2 R lmax lsub ex "
                 "mx ix esum rec wraw oh s1 s2 rank rsel p1 pos psel red kept slotk slots tags").split()
        S = {n: sem("a_" + n) for n in names}
        d_sc = [sem(f"d_sc{i}") for i in range(R)]
        t_names = "cnt_ps cnt cnt2 more nblk cum done0 done1 table table2 rows_ps rows tables"
        T = {n: sem("t_" + n) for n in t_names.split()}
        d_tail, d_ptail = sem("d_tail"), sem("d_ptail")
        d_xe = [sem(f"d_xe{i}") for i in range(U)]
        d_ye = [sem(f"d_ye{i}") for i in range(U)]
        NS = 4
        B = {n: [sem(f"b_{n}{u}") for u in range(NS)] for n in "ew xeT_ps xeT gu_ps sg hT y_ps ye second dst".split()}
        b_eturn = sem("b_eturn")
        b_held = sem("b_held")
        y_all = sem("y_all")
        d_yg = [sem(f"d_yg{g}") for g in range(NT // G)]
        f_sum, f_out = sem("f_sum"), sem("f_out")
        p_mul, p_sum, p_out = sem("p_mul"), sem("p_sum"), sem("p_out")
        d_out = sem("d_out")

        def need(eng, s, n):
            if n > 0:
                eng.wait_ge(s, n)

        block = ctx.enter_context(nc.Block())
        x_t = x.rearrange("b (t p) d -> p (b t) d", p=P)
        y2_t = y2.rearrange("(t p) d -> p t d", p=P)
        out_t = out.rearrange("b (t p) d -> p (b t) d", p=P)
        XQ = NT // 4

        def run(steps, order):
            for s in steps:
                for stage, lag in order:
                    if 0 <= s - lag < NB:
                        stage(s - lag)

        STEPS = range(-1, NB + 7)
        EARLY_FIRSTS = {-1: (0, 1, 2), 0: (3, 4), 1: (5, 6, 7)}
        EARLY_BIAS = {-1: (0,), 2: (1,), 3: (2,), 4: (3,)}

        SPT, POOLT = E * 7 // 16, E * 14 // 16

        def write_tails(eng, experts, signal):
            eng.wait_ge(T["more"], 1)
            _, rows = nc.values_load_multi_w_load_instructions(
                tail_i[0:1, experts[0]:experts[-1] + 1], engines=[eng.engine], min_val=0, max_val=SPARE - BLK,
                skip_runtime_bounds_check_because="an expert keeps K * CAP rows at most of its PITCH")
            for r in rows:
                eng.dma_start(xbuf[bass.ds(r, BLK), :], tailrows[:, :]).then_inc(signal, 16)

        def table_of(eng, tab, i, last):
            at = tab[0:1, U * i:U * i + U] if isinstance(i, int) else tab[0:1, bass.ds(U * i, U)]
            return nc.values_load_multi_w_load_instructions(
                at, engines=[eng.engine], min_val=0, max_val=last,
                skip_runtime_bounds_check_because="DVE makes the table from the experts' numbers and PITCH")[1]

        def done_of(eng, name, counts, u, back):
            v = u - back
            if counts[v // NS] is not None:
                eng.wait_ge(B[name][v % NS], counts[v // NS])

        def counts_of(eng, i, turns_back=range(-1, U // NS)):
            if isinstance(i, int):
                return {q: i * (U // NS) + q + 1 if i * (U // NS) + q + 1 > 0 else None for q in range(-U // NS, U // NS)}
            return {q: eng.snap(i * (U // NS) + (q + 1)) for q in turns_back}

        def of_pool(j):
            return j % G == G - 1

        def add_choice(k, j, signal):
            nc.vector.scalar_tensor_tensor(out=(ysum if k == 0 else xa)[:, j, :], in0=yg[:, k, j, :], scalar=wts[:, j, k:k + 1],
                                           in1=(xa if k == 0 else ysum)[:, j, :], op0=ALU.mult, op1=ALU.add).then_inc(signal, 1)

        @block.sync
        def _(sp):
            sp.dma_start(xs[:, 0:XQ, :], x_t[:, 0:XQ, :]).then_inc(d_x[0], 16)
            sp.dma_start(wqkv_sb[:, :, :], w_qkv.rearrange("(c p) d -> p c d", p=P)).then_inc(d_w, 16)
            sp.dma_start(wout_sb[:, :], w_out).then_inc(d_w, 16)
            sp.dma_start(rw_sb[:, :], router_w).then_inc(d_w, 16)
            sp.dma_start(brow[0:1, :], b_out.rearrange("(a d) -> a d", a=1)).then_inc(d_w, 16)
            for i in range(1, 4):
                sp.dma_start(xs[:, i * XQ:(i + 1) * XQ, :], x_t[:, i * XQ:(i + 1) * XQ, :]).then_inc(d_x[i], 16)
            sp.dma_start(ew_sb[:, 0:E, 0:D], gate_w.rearrange("e d h -> d e h")).then_inc(d_ew, 16)
            sp.dma_start(ew_sb[:, 0:E, D:2 * D], up_w.rearrange("e d h -> d e h")).then_inc(d_ew, 16)
            sp.dma_start(ew_sb[:, 0:E, 2 * D:], down_w.rearrange("e h d -> h e d")).then_inc(d_ew, 16)
            sp.wait_ge(c_pool, 2)
            sp.wait_ge(c_tail, 2)
            for i in range(SPARES):
                sp.dma_start(xbuf[SPARE + i * BLK:SPARE + (i + 1) * BLK, :], tailrows[:, :]).then_inc(d_spare, 16)
            sp.dma_start(y2.rearrange("(p r) d -> p r d", p=P),
                         zeros[:, :].unsqueeze(1).to_broadcast([P, K * NTOK // P, D])).then_inc(d_zero, 16)
            write_tails(sp, range(0, SPT), d_tail)
            sp.wait_ge(T["rows"], 1)
            turns = sp.value_load(turns_i[0:1, 0:1], min_val=0, max_val=MAXN // U - MINTURNS) + MINTURNS
            sp.wait_ge(d_spare, 16 * SPARES)
            sp.wait_ge(d_tail, 16 * POOLT)
            sp.wait_ge(d_ptail, 16 * (E - POOLT))
            for i in range(R):
                sp.wait_ge(d_sc[i], 16 * TB * K * len(range(i, NB, R)))

            def load_turn(i, counts):
                rows = table_of(sp, row_i, i, DROPPED - BLK)
                for u in range(U):
                    done_of(sp, "xeT_ps", counts, u, U)
                    if not isinstance(i, int):
                        sp.sem_inc(b_held, 1)
                    done_of(sp, "dst", counts, u, U)
                    sp.dma_start(xe[:, u, :], xbuf[bass.ds(rows[u], BLK), :]).then_inc(d_xe[u], 16)

            load_turn(0, counts_of(sp, 0))
            with sp.Fori(1, turns) as i:
                load_turn(i, counts_of(sp, i, range(-U // NS, 0)))
            sp.wait_ge(y_all, 1)
            for g in range(NT // G):
                sp.dma_start(yg[:, 0, G * g:G * g + G, :], y2_t[:, G * g:G * g + G, :]).then_inc(d_yg[g], 16)
            for g in range(NT // G):
                sp.wait_ge(f_out, (G - 1) * (g + 1))
                sp.wait_ge(p_out, g + 1)
                sp.dma_start(out_t[:, G * g:G * g + G, :], xa[:, G * g:G * g + G, :]).then_inc(d_out, 16)
            sp.wait_ge(d_out, 16 * (NT // G))

        @block.gpsimd
        def _(pool):
            nc.gpsimd.memset(zeros[:, :], 0.0).then_inc(c_pool, 1)
            nc.gpsimd.memset(tailrows[:, :], 0.0).then_inc(c_pool, 1)
            nc.gpsimd.memset(ident[:, :], 0.0).then_inc(c_pool, 1)
            nc.gpsimd.memset(tri_f[:, :], 1.0).then_inc(c_pool, 1)
            nc.gpsimd.memset(minus_half[:, :], -0.5).then_inc(c_pool, 1)
            nc.gpsimd.iota(iota_i[:, 0, :], pattern=[[1, E]], base=0, channel_multiplier=0).then_inc(c_pool, 1)
            nc.gpsimd.iota(iota_i[:, 1, :], pattern=[[PITCH, E]], base=0, channel_multiplier=0).then_inc(c_pool, 1)
            nc.gpsimd.iota(tok_i[:, :], pattern=[[P, NT]], base=0, channel_multiplier=1).then_inc(c_pool, 1)
            nc.gpsimd.iota(part_i[:, :], pattern=[[0, 1]], base=0, channel_multiplier=1).then_inc(c_pool, 1)
            nc.gpsimd.iota(steps_i[:, :], pattern=[[BLK, MAXB]], base=0, channel_multiplier=0).then_inc(c_pool, 1)
            pool.wait_ge(c_pool, 10)
            nc.gpsimd.memset(tailrows[:, FIRST:FIRST + 1], -1.0).then_inc(c_tail, 1)
            nc.gpsimd.memset(tailrows[:, TOKEN:TOKEN + 1], float(K * NTOK)).then_inc(c_tail, 1)
            nc.gpsimd.affine_select(out=ident[:, :], in_=ident[:, :], compare_op=ALU.not_equal, fill=1.0,
                                    base=0, pattern=[[-1, P]], channel_multiplier=1).then_inc(c_pool, 1)
            nc.gpsimd.affine_select(out=tri_f[:, :], in_=tri_f[:, :], compare_op=ALU.is_gt, fill=0.0,
                                    base=0, pattern=[[1, P]], channel_multiplier=-1).then_inc(c_pool, 1)

            def first_deviations(c):
                t0, t1 = TB * FIRSTS[c], TB * FIRSTS[c + 1]
                pool.wait_ge(S["ve1"], c + 1)
                nc.gpsimd.tensor_tensor(rs1[:, t0:t1], ve1[:, t0:t1], minus_half[:, t0:t1], ALU.pow).then_inc(S["rs1"], 1)

            def deviations_of(g):
                pool.wait_ge(S["ve2"], g + 1)
                c = slice(g % R * TB, g % R * TB + TB)
                nc.gpsimd.tensor_tensor(rs2[:, c], ve2[:, c], minus_half[:, c], ALU.pow).then_inc(S["rs2"], 1)

            def add_bias(c):
                pool.wait_ge(c_wc, 1)
                pool.wait_ge(d_x[c], 16)
                nc.gpsimd.tensor_tensor(xa[:, c * XQ:(c + 1) * XQ, :], xs[:, c * XQ:(c + 1) * XQ, :],
                                        bias_bc[:, :].unsqueeze(1).to_broadcast([P, XQ, D]), ALU.add).then_inc(S["xb"], 1)

            def scatter_rows(c):
                def stage(g):
                    if c == 0:
                        pool.wait_ge(S["slots"], g + 1)
                        pool.wait_ge(S["tags"], g + 1)
                    j = c // K
                    col = (TB * g + j) * K + c % K
                    nc.gpsimd.indirect_dma_start(
                        out=xbuf, out_offset=bass.IndirectOffsetOnAxis(ap=slots[:, col:col + 1], axis=0),
                        in_=xf[:, g % R, j, :], in_offset=None,
                        bounds_check=SPARE - 1, oob_is_err=False).then_inc(d_sc[g % R], 16)
                return stage

            for s in STEPS:
                run([s], [(deviations_of, 3)])
                for c in EARLY_FIRSTS.get(s, ()):
                    first_deviations(c)
                for c in EARLY_BIAS.get(s, ()):
                    add_bias(c)
                run([s], [(scatter_rows(c), 5) for c in range(TB * K)])

            write_tails(pool, range(POOLT, E), d_ptail)
            pool.wait_ge(T["tables"], 1)
            turns = pool.value_load(turns_i[0:1, 0:1], min_val=0, max_val=MAXN // U - MINTURNS) + MINTURNS
            pool.wait_ge(d_zero, 16)

            with pool.Fori(0, turns) as i:
                counts = counts_of(pool, i, range(U // NS))
                for u in range(U):
                    done_of(pool, "ye", counts, u, 0)
                    pool.sem_inc(b_held, 1)
                    nc.gpsimd.indirect_dma_start(
                        out=y2, out_offset=bass.IndirectOffsetOnAxis(ap=dst[:, u:u + 1], axis=0),
                        in_=ye[:, u, :], in_offset=None,
                        bounds_check=K * NTOK - 1, oob_is_err=False).then_inc(d_ye[u], 16)
            for u in range(U):
                pool.wait_ge(d_ye[u], 16 * turns)
                pool.sem_inc(b_held, 1)
            pool.sem_inc(y_all, 1)
            mine = [j for j in range(NT) if of_pool(j)]
            for n, j in enumerate(mine):
                pool.wait_ge(p_mul, n + 1)
                nc.gpsimd.tensor_tensor(ysum[:, j, :], yg[:, 0, j, :], xa[:, j, :], ALU.add).then_inc(p_sum, 1)
                pool.wait_ge(p_sum, n + 1)
                nc.gpsimd.tensor_tensor(xa[:, j, :], yg[:, 1, j, :], ysum[:, j, :], ALU.add).then_inc(p_out, 1)

        @block.scalar
        def _(act):
            act.wait_ge(c_w, 1)
            nc.scalar.activation(wqT[:, :], banks[0][:, 0:D], ACT.Copy)
            nc.scalar.activation(wkT[:, :], banks[0][:, D:2 * D], ACT.Copy)
            nc.scalar.activation(woT[:, :], banks[0][:, 2 * D:3 * D], ACT.Copy)
            nc.scalar.activation(bias_bc[:, :], banks[0][:, 3 * D:4 * D], ACT.Copy).then_inc(c_wc, 1)

            def cast(name, src, g, out, psum):
                act.wait_ge(S[src], g + 1)
                nc.scalar.activation(out, psum, ACT.Copy).then_inc(S[name], 1)

            def xn_of(q):
                act.wait_ge(S["nb1"], next(c for c in range(1, len(FIRSTS)) if q < FIRSTS[c]))
                for j in range(TB):
                    t = TB * q + j
                    ins = nc.scalar.activation(xn[:, q % R, j, :], xs[:, t, :], ACT.Identity,
                                               bias=nb1[:, t:t + 1], scale=rs1[:, t:t + 1])
                ins.then_inc(S["xn"], 1)

            def xnT_copy(q):
                cast("cT", "T", q, xnT[:, q % R, :], banks[0][:, 0:N])

            def relu(q):
                act.wait_ge(S["QK"], q + 1)
                nc.scalar.activation(qk[:, q % R, :], banks[1][:, :], ACT.Relu).then_inc(S["qr"], 1)

            def relu_eps(q):
                act.wait_ge(S["qr"], q + 1)
                nc.scalar.activation(qk[:, q % R, :], qk[:, q % R, :], ACT.Identity, bias=eps_col[:, :]).then_inc(S["qk"], 1)

            def g_copy(q):
                cast("gT", "G", q, gs[:, q % R, 0:D + 1], banks[2][:, 0:D + 1])

            def m_copy(q):
                cast("ms", "M", q, gs[:, q % R, D + 1:], banks[3][:, 0:D])

            def xf_of(g):
                act.wait_ge(S["nb2"], g + 1)
                if g >= R:
                    act.wait_ge(d_sc[g % R], 16 * TB * K * (g // R))
                for j in range(TB):
                    r = g % R * TB + j
                    ins = nc.scalar.activation(xf[:, g % R, j, 0:D], xa[:, TB * g + j, :], ACT.Identity,
                                               bias=nb2[:, r:r + 1], scale=rs2[:, r:r + 1])
                ins.then_inc(S["xf"], 1)

            def xfT_copy(g):
                cast("cT2", "T2", g, xfT[:, g % R, :], banks[5][:, 0:N])

            def exponent(g):
                act.wait_ge(S["lsub"], g + 1)
                nc.scalar.activation(ex[:, g % R, :, :], lsub[:, g % R, :, :], ACT.Exp).then_inc(S["ex"], 1)

            def tags(g):
                act.wait_ge(S["ix"], g + 1)
                nc.scalar.activation(xf[:, g % R, :, FIRST], tix[:, g % R, :, 0], ACT.Copy)
                nc.scalar.activation(xf[:, g % R, :, TOKEN], tok_f[:, TB * g:TB * g + TB], ACT.Copy).then_inc(S["tags"], 1)

            act.wait_ge(c_dve, 15)
            order = [(xn_of, -1), (relu, 1), (m_copy, 2), (relu_eps, 1), (exponent, 4), (xnT_copy, 0), (xf_of, 3), (g_copy, 1),
                     (xfT_copy, 3), (tags, 4)]
            run([-1], order)
            act.wait_ge(c_w, 2)
            nc.scalar.activation(wvo[:, :], banks[2][:, 0:D], ACT.Copy).then_inc(c_wc, 1)
            run(STEPS[1:], order)

            act.wait_ge(S["tags"], NB)
            nc.scalar.activation(warm[:, :], eps_col[:, :], ACT.Silu)
            write_tails(act, range(SPT, POOLT), d_tail)
            act.wait_ge(T["tables"], 1)
            turns = act.value_load(turns_i[0:1, 0:1], min_val=0, max_val=MAXN // U - MINTURNS) + MINTURNS

            def xeT_copy(counts, u):
                done_of(act, "xeT_ps", counts, u, 0)
                nc.scalar.activation(xeT[:, u % 2, :], banks[u % 2][:, 0:P], ACT.Copy).then_inc(B["xeT"][u % NS], 1)

            def silu(counts, u):
                v = (u - 1) % U
                done_of(act, "gu_ps", counts, u, 1)
                nc.scalar.activation(sg[:, v % 2, :], banks[2 + v % 2][:, 0:P], ACT.Silu).then_inc(B["sg"][v % NS], 1)

            def y_copy(counts, u, scattered):
                v = (u - 2) % U
                done_of(act, "y_ps", counts, u, 2)
                if scattered is not None:
                    act.wait_ge(d_ye[v], scattered)
                nc.scalar.activation(ye[:, v, :], banks[4 + v % 2][:, 0:D], ACT.Copy).then_inc(B["ye"][v % NS], 1)

            counts = counts_of(act, 0)
            for u in range(U):
                xeT_copy(counts, u)
                if u >= 1:
                    silu(counts, u)
                if u >= 2:
                    y_copy(counts, u, None)

            def turn(counts, earlier, before):
                for u in range(U):
                    xeT_copy(counts, u)
                    silu(counts, u)
                    y_copy(counts, u, earlier if u >= 2 else before)

            turn(counts_of(act, 1), 16, None)
            with act.Fori(2, turns) as i:
                turn(counts_of(act, i), act.snap(16 * i), act.snap(16 * i - 16))
            last = counts_of(act, turns, range(-1, 0))
            silu(last, 0)
            y_copy(last, 0, 16 * turns - 16)
            y_copy(last, 1, 16 * turns - 16)
            act.wait_ge(y_all, 1)
            for g in range(NT // G):
                act.dma_start(yg[:, 1, G * g:G * g + G, :], y2_t[:, NT + G * g:NT + G * g + G, :]).then_inc(d_yg[g], 16)
            for j in range(NT):
                if of_pool(j):
                    act.wait_ge(d_yg[j // G], 16 * K)
                    for k in range(K):
                        ins = nc.scalar.activation(yg[:, k, j, :], yg[:, k, j, :], ACT.Copy, scale=wts[:, j, k:k + 1])
                    ins.then_inc(p_mul, 1)

        @block.vector
        def _(dve):
            dve.wait_ge(c_pool, 12)
            nc.vector.tensor_copy(before[:, :], tri_f[:, :]).then_inc(c_dve, 1)
            nc.vector.memset(ones_bf[:, :], 1.0).then_inc(c_dve, 1)
            nc.vector.memset(ones_row[:, :], 1.0).then_inc(c_dve, 1)
            nc.vector.memset(ones_col[:, :], 1.0).then_inc(c_dve, 1)
            nc.vector.memset(eps_col[:, :], ATT_EPS).then_inc(c_dve, 1)
            nc.vector.tensor_copy(iota_e[:, :], iota_i[:, 0, :]).then_inc(c_dve, 1)
            nc.vector.tensor_copy(base_e[:, :], iota_i[:, 1, :]).then_inc(c_dve, 1)
            nc.vector.tensor_copy(tok_f[:, :], tok_i[:, :]).then_inc(c_dve, 1)
            nc.vector.tensor_copy(part[:, :], part_i[:, :]).then_inc(c_dve, 1)
            nc.vector.tensor_scalar(partrow[:, :], part_i[:, :], float(BLK), None, ALU.mult).then_inc(c_dve, 1)
            nc.vector.memset(xf[:, :, :, W - 2:W], 0.0).then_inc(c_dve, 1)
            nc.vector.tensor_copy(steps_f[:, :], steps_i[:, :]).then_inc(c_dve, 1)
            nc.vector.memset(seen[:, 0, 0, :, :], 0.0).then_inc(c_dve, 1)
            nc.vector.memset(ew_sb[:, E, :], 0.0).then_inc(c_dve, 1)
            nc.vector.memset(onesE[:, :], 1.0).then_inc(c_dve, 1)
            dve.wait_ge(c_dve, 15)

            def first_moments(c):
                t0, t1 = TB * FIRSTS[c], TB * FIRSTS[c + 1]
                for i in range(4):
                    if t0 <= i * XQ < t1 or i == t0 // XQ:
                        dve.wait_ge(d_x[i], 16)
                for t in range(t0, t1):
                    ins = nc.vector.bn_stats(st1[:, t, :], xs[:, t, :])
                ins.then_inc(S["st1"], 1)
                dve.wait_ge(S["st1"], c + 1)
                for t in range(t0, t1):
                    ins = nc.vector.bn_aggr(mv1[:, t, :], st1[:, t, :])
                ins.then_inc(S["ag1"], 1)
                dve.wait_ge(S["ag1"], c + 1)
                nc.vector.tensor_scalar(ve1[:, t0:t1], mv1[:, t0:t1, 1], LN_EPS, None, ALU.add).then_inc(S["ve1"], 1)

            def first_offsets(c):
                t0, t1 = TB * FIRSTS[c], TB * FIRSTS[c + 1]
                dve.wait_ge(S["rs1"], c + 1)
                nc.vector.scalar_tensor_tensor(out=nb1[:, t0:t1], in0=mv1[:, t0:t1, 0], scalar=-1.0, in1=rs1[:, t0:t1],
                                               op0=ALU.mult, op1=ALU.mult).then_inc(S["nb1"], 1)

            def nb_of(g):
                r = g % R
                dve.wait_ge(S["rs2"], g + 1)
                nc.vector.scalar_tensor_tensor(out=nb2[:, r * TB:r * TB + TB], in0=mv2[:, r, :, 0], scalar=-1.0,
                                               in1=rs2[:, r * TB:r * TB + TB], op0=ALU.mult, op1=ALU.mult).then_inc(S["nb2"], 1)

            def attention_sums(q):
                return banks[4][:, 0:TB * (D + 1)].rearrange("p (t d) -> p t d", t=TB)

            def den_of(q):
                dve.wait_ge(S["O"], q + 1)
                nc.vector.tensor_scalar(den[:, q % R, :], attention_sums(q)[:, :, 0], ATT_EPS, None, ALU.add).then_inc(S["den"], 1)

            def zz_of(q):
                dve.wait_ge(S["den"], q + 1)
                nc.vector.reciprocal(zz[:, q % R, :], den[:, q % R, :]).then_inc(S["zz"], 1)

            def x1_of(q):
                dve.wait_ge(S["zz"], q + 1)
                if q % (NB // 4) == 0:
                    dve.wait_ge(S["xb"], q // (NB // 4) + 1)
                for j in range(TB):
                    t = TB * q + j
                    ins = nc.vector.scalar_tensor_tensor(out=xa[:, t, :], in0=attention_sums(q)[:, j, 1:], scalar=zz[:, q % R, j:j + 1],
                                                         in1=xa[:, t, :], op0=ALU.mult, op1=ALU.add)
                ins.then_inc(S["x1"], 1)

            def st2_of(q):
                dve.wait_ge(S["x1"], q + 1)
                for j in range(TB):
                    ins = nc.vector.bn_stats(st2[:, q % R, j, :], xa[:, TB * q + j, :])
                ins.then_inc(S["st2"], 1)

            def ag2_of(q):
                dve.wait_ge(S["st2"], q + 1)
                for j in range(TB):
                    ins = nc.vector.bn_aggr(mv2[:, q % R, j, :], st2[:, q % R, j, :])
                ins.then_inc(S["ag2"], 1)

            def ve2_of(q):
                dve.wait_ge(S["ag2"], q + 1)
                nc.vector.tensor_scalar(ve2[:, q % R * TB:q % R * TB + TB], mv2[:, q % R, :, 1], LN_EPS, None,
                                        ALU.add).then_inc(S["ve2"], 1)

            def logits():
                return banks[6][:, 0:TB * E].rearrange("p (t e) -> p t e", t=TB)

            def lmax_of(g):
                dve.wait_ge(S["R"], g + 1)
                nc.vector.reduce_max(lmax[:, g % R, :], logits(), AX).then_inc(S["lmax"], 1)

            def lsub_of(g):
                dve.wait_ge(S["lmax"], g + 1)
                nc.vector.tensor_tensor(lsub[:, g % R, :, :], logits(), lmax[:, g % R, :].unsqueeze(2).to_broadcast([P, TB, E]),
                                        ALU.subtract).then_inc(S["lsub"], 1)

            def top_of(g):
                dve.wait_ge(S["ex"], g + 1)
                for j in range(TB):
                    ins = nc.vector.max(top[:, g % R, j, :], ex[:, g % R, j, :])
                ins.then_inc(S["mx"], 1)

            def index_of(g):
                dve.wait_ge(S["mx"], g + 1)
                for j in range(TB):
                    ins = nc.vector.max_index(tix[:, g % R, j, :], top[:, g % R, j, :], ex[:, g % R, j, :])
                ins.then_inc(S["ix"], 1)

            def esum_of(g):
                nc.vector.reduce_sum(esum[:, g % R, :], ex[:, g % R, :, :], AX).then_inc(S["esum"], 1)

            def rsum_of(g):
                dve.wait_ge(S["esum"], g + 1)
                nc.vector.reciprocal(rsum[:, g % R, :], esum[:, g % R, :]).then_inc(S["rec"], 1)

            def wraw_of(g):
                dve.wait_ge(S["rec"], g + 1)
                nc.vector.tensor_tensor(wraw[:, g % R, :, :], top[:, g % R, :, 0:K],
                                        rsum[:, g % R, :].unsqueeze(2).to_broadcast([P, TB, K]), ALU.mult).then_inc(S["wraw"], 1)

            def onehot_of(g):
                dve.wait_ge(S["ix"], g + 1)
                nc.vector.tensor_tensor(oh[:, TB * g:TB * g + TB, :, :],
                                        iota_e[:, :].unsqueeze(1).unsqueeze(1).to_broadcast([P, TB, K, E]),
                                        tix[:, g % R, :, 0:K].unsqueeze(3).to_broadcast([P, TB, K, E]),
                                        ALU.is_equal).then_inc(S["oh"], 1)

            def seen_first(g):
                dve.wait_ge(S["oh"], g + 1)
                need(dve, S["s2"], g)
                nc.vector.tensor_tensor(seen[:, g % R, 1, :, :], seen[:, g % R, 0, :, :], oh[:, TB * g, :, :],
                                        ALU.add).then_inc(S["s1"], 1)

            def seen_second(g):
                dve.wait_ge(S["s1"], g + 1)
                nc.vector.tensor_tensor(seen[:, (g + 1) % R, 0, :, :], seen[:, g % R, 1, :, :], oh[:, TB * g + 1, :, :],
                                        ALU.add).then_inc(S["s2"], 1)

            def place(g):
                dve.wait_ge(S["rank"], g + 1)
                rk = banks[7][:, 0:TB * K * E].rearrange("p (t k e) -> p t k e", t=TB, k=K)
                nc.vector.tensor_tensor(sel[:, g % R, 0, :, :, :], rk, oh[:, TB * g:TB * g + TB, :, :], ALU.mult).then_inc(S["rsel"], 1)
                nc.vector.scalar_tensor_tensor(out=p1[:, g % R, :, :], in0=rk[:, :, 1, :], scalar=float(CAP),
                                               in1=base_e[:, :].unsqueeze(1).to_broadcast([P, TB, E]),
                                               op0=ALU.min, op1=ALU.add).then_inc(S["p1"], 1)
                dve.wait_ge(S["p1"], g + 1)
                nc.vector.scalar_tensor_tensor(out=pos[:, g % R, :, :], in0=rk[:, :, 0, :], scalar=float(CAP),
                                               in1=p1[:, g % R, :, :], op0=ALU.min, op1=ALU.add).then_inc(S["pos"], 1)

            def psel_of(g):
                dve.wait_ge(S["pos"], g + 1)
                nc.vector.tensor_tensor(sel[:, g % R, 1, :, :, :], pos[:, g % R, :, :].unsqueeze(2).to_broadcast([P, TB, K, E]),
                                        oh[:, TB * g:TB * g + TB, :, :], ALU.mult).then_inc(S["psel"], 1)

            def red_of(g):
                dve.wait_ge(S["rsel"], g + 1)
                dve.wait_ge(S["psel"], g + 1)
                nc.vector.reduce_sum(rank_slot[:, g % R, :, :, :], sel[:, g % R, :, :, :, :], AX).then_inc(S["red"], 1)

            def kept_of(g):
                dve.wait_ge(S["red"], g + 1)
                nc.vector.tensor_scalar(kept[:, TB * g:TB * g + TB, :], rank_slot[:, g % R, 0, :, :], float(CAP), None,
                                        ALU.is_lt).then_inc(S["kept"], 1)

            def slotk_of(g):
                dve.wait_ge(S["kept"], g + 1)
                nc.vector.scalar_tensor_tensor(out=slotk[:, g % R, :, :], in0=rank_slot[:, g % R, 1, :, :], scalar=float(-DROPPED),
                                               in1=kept[:, TB * g:TB * g + TB, :], op0=ALU.add, op1=ALU.mult).then_inc(S["slotk"], 1)

            def slots_of(g):
                dve.wait_ge(S["slotk"], g + 1)
                nc.vector.tensor_scalar(slots[:, TB * K * g:TB * K * (g + 1)],
                                        slotk[:, g % R, :, :].rearrange("p t k -> p (t k)"), float(DROPPED), None,
                                        ALU.add).then_inc(S["slots"], 1)

            def wts_of(g):
                dve.wait_ge(S["wraw"], g + 1)
                nc.vector.tensor_tensor(wts[:, TB * g:TB * g + TB, :], wraw[:, g % R, :, :], kept[:, TB * g:TB * g + TB, :], ALU.mult)

            def kept_rows(g):
                if g == NB - 1:
                    dve.wait_ge(T["cnt_ps"], 1)
                    nc.vector.tensor_scalar(cnt[:, :], banks[2][:, 0:E], float(CAP), None, ALU.min).then_inc(T["cnt"], 1)
                    dve.wait_ge(T["cnt"], 1)
                    nc.vector.scalar_tensor_tensor(out=cnt2[:, :], in0=banks[2][:, E:2 * E], scalar=float(CAP), in1=cnt[:, :],
                                                   op0=ALU.min, op1=ALU.add).then_inc(T["cnt2"], 1)
                    dve.wait_ge(T["cnt2"], 1)
                    nc.vector.tensor_tensor(tail_i[:, :], cnt2[:, :], base_e[:, :], ALU.add).then_inc(T["more"], 1)

            for s in STEPS:
                for c in EARLY_FIRSTS.get(s, ()):
                    first_moments(c)
                    if c > 0:
                        first_offsets(c - 1)
                    if c == len(FIRSTS) - 2:
                        first_offsets(c)
                run([s], [(ag2_of, 3), (place, 5), (ve2_of, 3), (seen_second, 5), (esum_of, 5), (psel_of, 5), (rsum_of, 5), (red_of, 5),
                          (kept_rows, 5), (wraw_of, 5), (kept_of, 5), (slotk_of, 5), (wts_of, 5), (slots_of, 5), (lmax_of, 4),
                          (nb_of, 3), (lsub_of, 4), (den_of, 2), (top_of, 4), (zz_of, 2), (index_of, 4),
                          (x1_of, 2), (onehot_of, 4), (seen_first, 4), (st2_of, 2)])

            nc.vector.tensor_tensor(more[:, :, :], cnt2[:, :].unsqueeze(2).to_broadcast([P, E, MAXB]),
                                    steps_f[:, :].unsqueeze(1).to_broadcast([P, E, MAXB]), ALU.is_gt).then_inc(T["more"], 1)
            dve.wait_ge(T["more"], 2)
            nc.vector.reduce_sum(nblk[:, :], more[:, :, :], AX).then_inc(T["nblk"], 1)
            dve.wait_ge(T["nblk"], 1)
            nc.vector.tensor_tensor_scan(cum[:, :], onesE[:, :], nblk[:, :], 0.0, ALU.mult, ALU.add).then_inc(T["cum"], 1)
            dve.wait_ge(T["cum"], 1)
            nc.vector.tensor_scalar(done[:, 0, :], cum[:, :], part[:, 0:1], None, ALU.is_le).then_inc(T["done0"], 1)
            nc.vector.tensor_scalar(skip[:, :], nblk[:, :], float(-BLK), float(PITCH), ALU.mult, ALU.add).then_inc(T["done0"], 1)
            nc.vector.tensor_scalar(blocks[:, :], cum[:, E - 1:E], float(MINTURNS * U), None, ALU.max).then_inc(T["done0"], 1)
            dve.wait_ge(T["done0"], 3)
            nc.vector.tensor_tensor(done[:, 1, :], done[:, 0, :], skip[:, :], ALU.mult).then_inc(T["done1"], 1)
            nc.vector.tensor_scalar(turns_i[:, :], blocks[:, :], 1.0 / U, 0.5 - 0.5 / U - MINTURNS, ALU.mult, ALU.add)
            dve.wait_ge(T["done1"], 1)
            nc.vector.reduce_sum(table[:, :], done[:, :, :], AX).then_inc(T["table"], 1)
            dve.wait_ge(T["table"], 1)
            nc.vector.tensor_tensor(table2[:, :], table[:, 1:2], partrow[:, :], ALU.add).then_inc(T["table2"], 1)
            dve.wait_ge(T["rows_ps"], 1)
            nc.vector.tensor_copy(row_i[:, :], banks[5][0:1, P:2 * P]).then_inc(T["rows"], 1)
            nc.vector.tensor_copy(exp_i[:, :], banks[5][0:1, 0:P])
            nc.vector.tensor_copy(eblk[:, :], banks[5][:, 0:P]).then_inc(T["tables"], 1)
            dve.wait_ge(T["tables"], 1)
            turns = dve.value_load(turns_i[0:1, 0:1], min_val=0, max_val=MAXN // U - MINTURNS) + MINTURNS

            def weights(counts, u, e):
                done_of(dve, "y_ps", counts, u, U)
                if not isinstance(counts[0], int):
                    dve.sem_inc(b_held, 1)
                nc.vector.tensor_copy(ew[:, u, :], ew_sb[:, bass.ds(e, 1), :].rearrange("p o h -> p (o h)")).then_inc(B["ew"][u % NS], 1)

            def targets(counts, u, landed, scattered):
                dve.wait_ge(d_xe[u], landed)
                nc.vector.tensor_tensor(second[:, u:u + 1], xe[:, u, FIRST:FIRST + 1], eturn[:, u:u + 1],
                                        ALU.not_equal).then_inc(B["second"][u % NS], 1)
                done_of(dve, "second", counts, u, 0)
                if scattered is not None:
                    dve.wait_ge(d_ye[u], scattered)
                nc.vector.scalar_tensor_tensor(out=dst[:, u:u + 1], in0=second[:, u:u + 1], scalar=float(NTOK),
                                               in1=xe[:, u, TOKEN:TOKEN + 1], op0=ALU.mult, op1=ALU.add).then_inc(B["dst"][u % NS], 1)

            def hidden(counts, u):
                v = (u - 1) % U
                done_of(dve, "sg", counts, u, 1)
                nc.vector.tensor_tensor(hT[:, v % 2, :], sg[:, v % 2, :], banks[2 + v % 2][:, P:2 * P],
                                        ALU.mult).then_inc(B["hT"][v % NS], 1)

            def turn(i, counts, landed, scattered):
                experts = table_of(dve, exp_i, i, E)
                of_turn = eblk[:, 0:U] if isinstance(i, int) else eblk[:, bass.ds(U * i, U)]
                nc.vector.tensor_copy(eturn[:, :], of_turn).then_inc(b_eturn, 1)
                for u in range(U):
                    weights(counts, u, experts[u])
                    if u == 0:
                        dve.wait_ge(b_eturn, i + 1)
                        dve.sem_inc(b_held, 1)
                    targets(counts, u, landed, scattered)
                    if u >= 1 or not isinstance(i, int):
                        hidden(counts, u)

            dve.wait_ge(d_ew, 48)
            turn(0, counts_of(dve, 0), 16, None)
            with dve.Fori(1, turns) as i:
                turn(i, counts_of(dve, i, range(-U // NS, U // NS)), dve.snap(16 * i + 16), dve.snap(16 * i))
            hidden(counts_of(dve, turns, range(-1, 0)), 0)

            mine = [j for j in range(NT) if not of_pool(j)]
            for n in range(0, len(mine), 2):
                for j in mine[n:n + 2]:
                    dve.wait_ge(d_yg[j // G], 16 * K)
                    add_choice(0, j, f_sum)
                for i, j in enumerate(mine[n:n + 2]):
                    dve.wait_ge(f_sum, n + i + 1)
                    add_choice(1, j, f_out)

        @block.tensor
        def _(pe):
            mm = nc.tensor.matmul
            pe.wait_ge(c_pool, 1)
            for _ in range(WAKE):
                mm(banks[7][:, 0:D], zeros[:, :], zeros[:, :], start=True, stop=True)
            pe.wait_ge(c_pool, 11)
            pe.wait_ge(c_dve, 3)
            pe.wait_ge(d_w, 64)
            nc.tensor.transpose(banks[0][:, 0:D], wqkv_sb[:, 0, :], ident[:, :])
            nc.tensor.transpose(banks[0][:, D:2 * D], wqkv_sb[:, 1, :], ident[:, :])
            nc.tensor.transpose(banks[0][:, 2 * D:3 * D], wout_sb[:, :], ident[:, :])
            mm(banks[0][:, 3 * D:4 * D], ones_row[:, :], brow[:, :], start=True, stop=True).then_inc(c_w, 1)
            pe.wait_ge(c_wc, 1)
            mm(banks[2][:, 0:D], wqkv_sb[:, 2, :], woT[:, :], start=True, stop=True).then_inc(c_w, 1)
            pe.wait_ge(c_dve, 15)

            def rank_of(g):
                pe.wait_ge(S["s1"], g + 1)
                need(pe, S["rsel"], g)
                need(pe, S["pos"], g)
                r = banks[7][:, 0:TB * K * E]
                mm(r, before[:, :], oh[:, TB * g:TB * g + TB, :, :].rearrange("p t k e -> p (t k e)"), start=True, stop=False)
                mm(r, ones_bf[:, :], seen[:, g % R, :, :, :].rearrange("p t k e -> p (t k e)"), start=False, stop=True).then_inc(S["rank"], 1)

            def transposes(bank, src, name):
                for j in range(TB):
                    ins = nc.tensor.transpose(banks[bank][:, j * P:(j + 1) * P], src(j), ident[:, :])
                ins.then_inc(S[name], 1)

            def xn_transposed(q):
                pe.wait_ge(S["xn"], q + 1)
                need(pe, S["cT"], q)
                transposes(0, lambda j: xn[:, q % R, j, :], "T")

            def qk_of(q):
                pe.wait_ge(S["cT"], q + 1)
                need(pe, S["qr"], q)
                for j in range(TB):
                    mm(banks[1][:, N + j * D:N + (j + 1) * D], xnT[:, q % R, j * P:(j + 1) * P], wkT[:, :], start=True, stop=True)
                mm(banks[1][:, 0:N], wqT[:, :], xnT[:, q % R, :], start=True, stop=True).then_inc(S["QK"], 1)

            def g_of(q):
                if q == 0:
                    pe.wait_ge(c_wc, 2)
                pe.wait_ge(S["qk"], q + 1)
                need(pe, S["gT"], q)
                k = qk[:, q % R, N:].rearrange("p (t d) -> p t d", t=TB)
                for j in range(TB):
                    mm(banks[2][:, 0:D], xn[:, q % R, j, :], k[:, j, :], start=(j == 0), stop=(j == TB - 1))
                for j in range(TB):
                    ins = mm(banks[2][:, D:2 * D], k[:, j, :], ones_col[:, :].to_broadcast([P, D]), start=(j == 0), stop=(j == TB - 1))
                ins.then_inc(S["G"], 1)

            def m_of(q):
                if q == 0:
                    pe.wait_ge(c_wc, 2)
                pe.wait_ge(S["gT"], q + 1)
                need(pe, S["ms"], q)
                mm(banks[3][:, 0:D], gs[:, q % R, 0:D], wvo[:, :], start=True, stop=True).then_inc(S["M"], 1)

            def o_of(q):
                pe.wait_ge(S["ms"], q + 1)
                need(pe, S["x1"], q)
                for j in range(TB):
                    ins = mm(banks[4][:, j * (D + 1):(j + 1) * (D + 1)], qk[:, q % R, j * P:(j + 1) * P], gs[:, q % R, D:],
                             start=True, stop=True)
                ins.then_inc(S["O"], 1)

            def xf_transposed(g):
                pe.wait_ge(S["xf"], g + 1)
                need(pe, S["cT2"], g)
                transposes(5, lambda j: xf[:, g % R, j, 0:D], "T2")

            def logits_of(g):
                pe.wait_ge(S["cT2"], g + 1)
                need(pe, S["lsub"], g)
                for j in range(TB):
                    ins = mm(banks[6][:, j * E:(j + 1) * E], xfT[:, g % R, j * P:(j + 1) * P], rw_sb[:, :], start=True, stop=True)
                ins.then_inc(S["R"], 1)

            run(STEPS, [(rank_of, 5), (qk_of, 1), (m_of, 2), (logits_of, 4), (xn_transposed, 0), (o_of, 2), (g_of, 1),
                        (xf_transposed, 3)])

            pe.wait_ge(S["gT"], NB)
            pe.wait_ge(S["s2"], NB)
            mm(banks[2][:, 0:K * E], ones_bf[:, :], seen[:, NB % R, 0, :, :].rearrange("p k e -> p (k e)"),
               start=True, stop=True).then_inc(T["cnt_ps"], 1)
            for src, ready, c in ((table[:, 0:1], "table", 0), (table2[:, 0:1], "table2", 1)):
                pe.wait_ge(T[ready], 1)
                ins = mm(banks[5][:, c * P:(c + 1) * P], src.to_broadcast([P, P]), ident[:, :], start=True, stop=True)
            ins.then_inc(T["rows_ps"], 1)
            pe.wait_ge(T["rows"], 1)
            turns = pe.value_load(turns_i[0:1, 0:1], min_val=0, max_val=MAXN // U - MINTURNS) + MINTURNS

            def transpose_in(counts, u, landed):
                pe.wait_ge(d_xe[u], landed)
                done_of(pe, "xeT", counts, u, 2)
                nc.tensor.transpose(banks[u % 2][:, 0:P], xe[:, u, 0:D], ident[:, :]).then_inc(B["xeT_ps"][u % NS], 1)

            def gate_up(counts, u):
                v = (u - 1) % U
                done_of(pe, "xeT", counts, u, 1)
                done_of(pe, "ew", counts, u, 1)
                done_of(pe, "hT", counts, u, 3)
                for c in range(2):
                    ins = mm(banks[2 + v % 2][:, c * P:(c + 1) * P], ew[:, v, c * D:(c + 1) * D], xeT[:, v % 2, :],
                             start=True, stop=True)
                ins.then_inc(B["gu_ps"][v % NS], 1)

            def down(counts, u):
                v = (u - 2) % U
                done_of(pe, "hT", counts, u, 2)
                done_of(pe, "ye", counts, u, 4)
                mm(banks[4 + v % 2][:, 0:D], hT[:, v % 2, :], ew[:, v, 2 * D:], start=True, stop=True).then_inc(B["y_ps"][v % NS], 1)

            counts = counts_of(pe, 0)
            for u in range(U):
                transpose_in(counts, u, 16)
                if u >= 1:
                    gate_up(counts, u)
                if u >= 2:
                    down(counts, u)
            with pe.Fori(1, turns) as i:
                counts, landed = counts_of(pe, i), pe.snap(16 * i + 16)
                for u in range(U):
                    transpose_in(counts, u, landed)
                    gate_up(counts, u)
                    down(counts, u)
            last = counts_of(pe, turns, range(-1, 0))
            gate_up(last, 0)
            down(last, 0)
            down(last, 1)


_INS = ['L0_attn_x', 'L0_attn_W_qkv', 'L0_attn_W_out', 'L0_attn_b_out', 'L0_ffn_router_w',
        'L0_ffn_gate_w', 'L0_ffn_up_w', 'L0_ffn_down_w']


def kernel(**inputs):
    import numpy as _np
    import concourse.bacc as _bacc
    from concourse import mybir as _mybir
    from concourse.bass_utils import run_bass_kernel_spmd as _run

    nc = _bacc.Bacc("TRN2", target_bir_lowering=False, num_devices=1)
    arrays, args = {}, []
    for name in _INS:
        a = _np.ascontiguousarray(inputs[name])
        arrays[f"in_{name}_dram"] = a
        args.append(nc.dram_tensor(f"in_{name}_dram", a.shape, _mybir.dt.from_np(a.dtype), kind="ExternalInput").ap())
    f32 = _mybir.dt.float32
    D = inputs['L0_attn_x'].shape[-1]
    E, K = inputs['L0_ffn_router_w'].shape[1], 2
    T = inputs['L0_attn_x'].shape[0] * inputs['L0_attn_x'].shape[1]
    _, blk, _, pitch, _, _, spares = sizes(T, E, K)
    rows = E * pitch + spares * blk
    xbuf = nc.dram_tensor("expert_rows", (rows, D + 4), f32).ap()
    y2 = nc.dram_tensor("expert_results", (K * T, D), f32).ap()
    out = nc.dram_tensor("out_0_dram", tuple(inputs['L0_attn_x'].shape), f32, kind="ExternalOutput").ap()
    linear_attention_moe(nc, *args, xbuf, y2, out)
    r = _run(nc, [arrays], core_ids=[0])
    return r.results[0]["out_0_dram"]
```
